# Optimizing a Trainium2 kernel written in Bass

```python
import numpy as np
import jax
import jax.numpy as jnp

def _softmax(x, axis=-1):
    return jax.nn.softmax(x, axis=axis)

def _gelu(x):
    return jax.nn.gelu(x, approximate=True)

def _silu(x):
    return jax.nn.silu(x)

def _sigmoid(x):
    return jax.nn.sigmoid(x)

def _layernorm(x, axis=-1, eps=1e-05):
    m = jnp.mean(x, axis=axis, keepdims=True)
    v = jnp.var(x, axis=axis, keepdims=True)
    return (x - m) / jnp.sqrt(v + eps)

def _scatter_add(tgt, idx, src, axis=0):
    return tgt.at[idx].add(src)

def _segment_sum(src, seg, n):
    return jax.ops.segment_sum(src, seg, n)
kernel_name = 'mk_adj_preln_d1_adj_r2_8a8af9'

def setup_inputs(seed: int=0):
    np.random.seed(seed)
    _w = jnp.asarray

    def _rec_inputs():
        import jax
        import jax.numpy as jnp
        _gk = jax.random.key(seed)
        x = -0.000929 + 1 * jax.random.normal(jax.random.fold_in(_gk, 1), (4096, 128), jnp.float32)
        _w = (1.0 + jnp.arange(4096, dtype=jnp.float32)) ** (-0.5)
        _w = _w / _w.mean()
        _pij = jnp.clip(0.00390625 * _w[:, None] * _w[None, :], 0.0, 1.0)
        _a = jax.random.uniform(jax.random.fold_in(_gk, 2), (4096, 4096)) < _pij
        _af = _a.astype(jnp.float32)
        _af = _af * jax.random.uniform(jax.random.fold_in(_gk, 3), (4096, 4096), jnp.float32, 0.05, 1)
        adj = _af
        return (x, adj)
    x, adj = _rec_inputs()

    def _L0_gnn_setup():
        import jax, jax.numpy as jnp
        import numpy as np
        N = 4096
        F_IN = 128
        F_OUT = 128
        ALPHA = 0.2
        NEG_INF = -9000000000000000.0

        def _signed_adj(key, n, p=0.002):
            r = jax.random.uniform(key, (n, n), dtype=jnp.float32)
            return jnp.where(r < p, 1.0, jnp.where(r > 1.0 - p, -1.0, 0.0)).astype(jnp.float32)
        key = jax.random.key(seed)
        k_h, k_na, k_ea, k_w, k_a = jax.random.split(key, 5)
        h = jax.random.normal(k_h, (N, F_IN), dtype=jnp.float32)
        node_adj = _signed_adj(k_na, N)
        edge_adj = _signed_adj(k_ea, N)
        lim_w = 1.414 * np.sqrt(6.0 / (F_IN + F_OUT))
        W = jax.random.uniform(k_w, (F_IN, F_OUT), dtype=jnp.float32, minval=-lim_w, maxval=lim_w)
        lim_a = 1.414 * np.sqrt(6.0 / (2 * F_OUT + 1))
        a = jax.random.uniform(k_a, (2 * F_OUT, 1), dtype=jnp.float32, minval=-lim_a, maxval=lim_a)
        return {'h': h, 'node_adj': node_adj, 'edge_adj': edge_adj, 'W': W, 'a': a}
    _L0_gnn_all = _L0_gnn_setup()
    _L0_gnn_in = {k: v for k, v in _L0_gnn_all.items() if k in ('W', 'a')}
    del _L0_gnn_all
    return {'x': x, 'adj': adj, 'L0_gnn_W': _L0_gnn_in['W'], 'L0_gnn_a': _L0_gnn_in['a']}

def reference(x, adj, L0_gnn_W, L0_gnn_a):
    import jax
    import jax.numpy as jnp

    def _L0_gnn_ref(h, node_adj, edge_adj, W, a):
        import jax, jax.numpy as jnp
        import numpy as np
        N = 4096
        F_IN = 128
        F_OUT = 128
        ALPHA = 0.2
        NEG_INF = -9000000000000000.0

        def _signed_adj(key, n, p=0.002):
            r = jax.random.uniform(key, (n, n), dtype=jnp.float32)
            return jnp.where(r < p, 1.0, jnp.where(r > 1.0 - p, -1.0, 0.0)).astype(jnp.float32)
        hw = h @ W
        pos = (node_adj > 0).astype(hw.dtype)
        neg = (node_adj < 0).astype(hw.dtype)
        h_plus = pos @ hw
        h_minus = neg @ hw
        a1, a2 = (a[:F_OUT], a[F_OUT:])
        e_plus = jax.nn.leaky_relu((h_plus @ a1 + h_minus @ a2)[:, 0], ALPHA)
        e_minus = jax.nn.leaky_relu((h_minus @ a1 + h_plus @ a2)[:, 0], ALPHA)
        scores = jnp.where(edge_adj > 0, e_plus[None, :], NEG_INF)
        scores = jnp.where(edge_adj < 0, e_minus[None, :], scores)
        attn = jax.nn.softmax(scores, axis=1)
        h_prime = attn * edge_adj @ hw
        return h_prime
    h = jnp.maximum(_layernorm(x, axis=-1), 0.0)
    x = x + _L0_gnn_ref(h, adj, adj, L0_gnn_W, L0_gnn_a)
    return x

_drawn_inputs = setup_inputs


def setup_inputs(seed=0):
    import zlib

    import numpy as np

    out = dict(_drawn_inputs(seed))
    spreads = {}
    factors = {}
    for name, (base, spread) in spreads.items():
        noise = np.random.default_rng([zlib.crc32(name.encode()), seed]).standard_normal(out[name].shape)
        drawn = base * np.exp(spread * noise) if base else spread * noise
        out[name] = jnp.asarray(drawn.astype(out[name].dtype))
    for name, factor in factors.items():
        out[name] = (out[name] * factor).astype(out[name].dtype)
    return out
```

```python
import numpy as np
import concourse.bass as bass
from concourse import mybir
from contextlib import ExitStack

P = 128


def build(nc, x, adj, W, a, out):
    fp32 = mybir.dt.float32
    ALU = mybir.AluOpType
    ACT = mybir.ActivationFunctionType
    AX = mybir.AxisListType

    N, F = x.shape
    T = N // P
    EPS = 1e-5
    ALPHA = 0.2
    BIG = 2.0 ** 53
    GRP = 4
    XG = 8

    x_rows = x.rearrange("(t p) f -> p t f", p=P)
    out_rows = out.rearrange("(t p) f -> p t f", p=P)
    adj_rows = adj.rearrange("(t p) n -> p t n", p=P)

    with ExitStack() as ctx:
        def sb(name, shape, dt=fp32):
            return ctx.enter_context(nc.sbuf_tensor(name, shape, dt))

        def sem(name):
            return ctx.enter_context(nc.semaphore(name))

        x_sb = sb("x_sb", [P, T, F])
        hw = sb("hw", [P, T, F])
        uv = sb("uv", [P, T, 2])
        ident = sb("ident", [P, P])
        ones = sb("ones", [P, P])
        W_aug = sb("W_aug", [P, F + 2])
        W_T = sb("W_T", [P, F])
        a_sb = sb("a_sb", [P, 2])
        stats = sb("stats", [P, T, 6])
        mv = sb("mv", [P, T, 2])
        var_eps = sb("var_eps", [P, T])
        std = sb("std", [P, T])
        rstd0 = sb("rstd0", [P, T])
        newton = sb("newton", [P, T])
        rstd = sb("rstd", [P, T])
        acc = sb("acc", [P, T, F])
        hT = sb("hT", [P, 2, GRP * P])

        bcast = sb("bcast", [P, 2, N])
        row = sb("row", [P, N])
        t1 = sb("t1", [P, N])
        t2 = sb("t2", [P, N])
        prob = sb("prob", [P, N])
        probT = acc[:, :, :].rearrange("p t f -> p (t f)")
        diag = sb("diag", [P, 2, P])
        part = sb("part", [P, 4])
        e_raw = sb("e_raw", [P, T, 2])
        e_sc = sb("e_sc", [P, T, 2])
        stat = sb("stat", [P, 4])
        out_t = sb("out_t", [P, F])

        ps = ctx.enter_context(nc.psum_tensor("ps", [P, 8, 512], fp32))

        x_loaded = [sem(f"x_loaded{g}") for g in range(T // XG)]
        w_loaded = sem("w_loaded")
        const_ready = sem("const_ready")
        ident_zero = sem("ident_zero")
        wT_done = sem("wT_done")
        wT_copied = sem("wT_copied")
        wa_done = sem("wa_done")
        wa_copied = sem("wa_copied")
        bn_done = sem("bn_done")
        var_ready = sem("var_ready")
        std_ready = sem("std_ready")
        dve = sem("dve")
        xn_ready = sem("xn_ready")
        hT_done = sem("hT_done")
        hT_copied = sem("hT_copied")
        hw_done = sem("hw_done")
        hw_copied = sem("hw_copied")
        g_diag = sem("g_diag")
        g_bc = sem("g_bc")
        g_bcc = sem("g_bcc")
        g_row = sem("g_row")
        g_rowused = sem("g_rowused")
        g_dve = sem("g_dve")
        g_t = sem("g_t")
        g_p = sem("g_p")
        g_q = sem("g_q")
        g_qT = sem("g_qT")
        g_qTc = sem("g_qTc")
        g_prod = sem("g_prod")
        g_out = sem("g_out")
        g_stored = sem("g_stored")

        NG = T // GRP
        NG = T // GRP
        block = ctx.enter_context(nc.Block())

        @block.sync
        def _(sp):
            for g in range(T // XG):
                sp.dma_start(x_sb[:, g * XG:(g + 1) * XG, :],
                             x_rows[:, g * XG:(g + 1) * XG, :]).then_inc(x_loaded[g], 16)
            with sp.Fori(0, T) as i:
                sp.wait_ge(g_rowused, i + 1)
                sp.dma_start(row[:, :], adj_rows[:, bass.ds(i, 1), :].rearrange("p a n -> p (a n)")).then_inc(g_row, 16)
            with sp.Fori(0, T) as i:
                sp.wait_ge(g_rowused, i + 1 + T)
                sp.dma_start(row[:, :], adj_rows[:, bass.ds(i, 1), :].rearrange("p a n -> p (a n)")).then_inc(g_row, 16)
                sp.wait_ge(g_out, i + 1)
                sp.dma_start(out_rows[:, bass.ds(i, 1), :], out_t[:, :].rearrange("p (a f) -> p a f", a=1)).then_inc(g_stored, 16)
            sp.wait_ge(g_stored, 16 * T)

        @block.gpsimd
        def _(pool):
            nc.gpsimd.memset(ident[:, :], 0.0).then_inc(ident_zero, 1)
            nc.gpsimd.memset(ones[:, :], 1.0).then_inc(const_ready, 1)
            pool.wait_ge(ident_zero, 1)
            nc.gpsimd.affine_select(out=ident[:, :], in_=ident[:, :], compare_op=ALU.not_equal, fill=1.0,
                                    base=0, pattern=[[-1, P]], channel_multiplier=1).then_inc(const_ready, 1)

        @block.scalar
        def _(act):
            act.dma_start(W_aug[:, 0:F], W[:, :]).then_inc(w_loaded, 16)
            for c in range(2):
                act.dma_start(a_sb[:, c:c + 1], a[c * F:(c + 1) * F, :]).then_inc(w_loaded, 16)
            act.wait_ge(wT_done, 1)
            nc.scalar.activation(W_T[:, :], ps[:, 0, 0:F], ACT.Copy).then_inc(wT_copied, 1)
            act.wait_ge(wa_done, 1)
            nc.scalar.activation(W_aug[:, F:F + 2], ps[:, 1, 0:2], ACT.Copy).then_inc(wa_copied, 1)
            act.wait_ge(var_ready, 1)
            nc.scalar.activation(std[:, :], var_eps[:, :], ACT.Sqrt).then_inc(std_ready, 1)
            for g in range(NG):
                act.wait_ge(hT_done, g + 1)
                if g >= 2:
                    act.wait_ge(hw_done, g - 1)
                nc.scalar.activation(hT[:, g % 2, :], ps[:, 2 + g % 2, :], ACT.Relu).then_inc(hT_copied, 1)
            with act.Fori(0, T) as i:
                act.wait_ge(g_t, i + 1)
                nc.scalar.activation(prob[:, :], t1[:, :], ACT.Exp, bias=stat[:, 1:2], scale=-BIG,
                                     accum_out=stat[:, 2:3]).then_inc(g_p, 1)
                for g in range(NG):
                    act.wait_ge(g_qT, i * NG + g + 1)
                    nc.scalar.activation(probT[:, g * 512:(g + 1) * 512], ps[:, g % 4, :],
                                         ACT.Copy).then_inc(g_qTc, 1)

        @block.tensor
        def _(pe):
            pe.wait_ge(const_ready, 2)
            pe.wait_ge(w_loaded, 48)
            nc.tensor.transpose(ps[:, 0, 0:F], W_aug[:, 0:F], ident[:, :]).then_inc(wT_done, 1)
            pe.wait_ge(wT_copied, 1)
            nc.tensor.matmul(ps[:, 1, 0:2], W_T[:, :], a_sb[:, :], start=True, stop=True).then_inc(wa_done, 1)
            pe.wait_ge(wa_copied, 1)

            def project(g):
                pe.wait_ge(hT_copied, g + 1)
                if g >= 2:
                    pe.wait_ge(hw_copied, g - 1)
                for k in range(GRP):
                    b = 4 + 2 * (g % 2) + k // 2
                    o = 256 * (k % 2)
                    mm = nc.tensor.matmul(ps[:, b, o:o + F + 2], hT[:, g % 2, k * P:(k + 1) * P], W_aug[:, :],
                                          start=True, stop=True)
                mm.then_inc(hw_done, 1)

            for g in range(NG):
                pe.wait_ge(xn_ready, g + 1)
                if g >= 2:
                    pe.wait_ge(hT_copied, g - 1)
                for k in range(GRP):
                    tr = nc.tensor.transpose(ps[:, 2 + g % 2, k * P:(k + 1) * P], acc[:, g * GRP + k, :], ident[:, :])
                tr.then_inc(hT_done, 1)
                if g >= 1:
                    project(g - 1)
            project(NG - 1)
            for r in range(2):
                with pe.Fori(0, T) as i:
                    pe.wait_ge(g_diag, i + 1 + r * T)
                    for c in range(2):
                        mm = nc.tensor.matmul(ps[:, c, 0:P], ones[:, :], diag[:, c, :], start=True, stop=True)
                    mm.then_inc(g_bc, 1)
            with pe.Fori(0, T) as i:
                pe.wait_ge(g_q, i + 1)
                for g in range(NG):
                    if g >= 4:
                        pe.wait_ge(g_qTc, i * NG + g - 3)
                    for k in range(GRP):
                        b = g * GRP + k
                        tr = nc.tensor.transpose(ps[:, g % 4, k * P:(k + 1) * P], t2[:, b * P:(b + 1) * P], ident[:, :])
                    tr.then_inc(g_qT, 1)
                pe.wait_ge(g_qTc, i * NG + NG)
                for b in range(T):
                    mm = nc.tensor.matmul(ps[:, 5, 0:F], probT[:, b * P:(b + 1) * P], hw[:, b, :],
                                          start=b == 0, stop=b == T - 1)
                mm.then_inc(g_prod, 1)

        @block.vector
        def _(v):
            n = 0

            def link(ins):
                nonlocal n
                n += 1
                ins.then_inc(dve, 1)
                v.wait_ge(dve, n)

            for g in range(T // XG):
                v.wait_ge(x_loaded[g], 16)
                for t in range(g * XG, (g + 1) * XG):
                    last = nc.vector.bn_stats(stats[:, t, :], x_sb[:, t, :])
            link(last)
            for t in range(T):
                last = nc.vector.bn_aggr(mv[:, t, :], stats[:, t, :])
            link(last)
            nc.vector.tensor_scalar(var_eps[:, :], mv[:, :, 1], EPS, None, ALU.add).then_inc(var_ready, 1)
            v.wait_ge(std_ready, 1)
            link(nc.vector.reciprocal(rstd0[:, :], std[:, :]))
            link(nc.vector.tensor_tensor(newton[:, :], rstd0[:, :], rstd0[:, :], ALU.mult))
            link(nc.vector.tensor_tensor(newton[:, :], newton[:, :], var_eps[:, :], ALU.mult))
            link(nc.vector.tensor_scalar(newton[:, :], newton[:, :], -0.5, 1.5, ALU.mult, ALU.add))
            link(nc.vector.tensor_tensor(rstd[:, :], rstd0[:, :], newton[:, :], ALU.mult))
            for g in range(NG):
                for t in range(g * GRP, (g + 1) * GRP):
                    last = nc.vector.tensor_scalar(acc[:, t, :], x_sb[:, t, :], mv[:, t, 0:1], rstd[:, t:t + 1],
                                                   ALU.subtract, ALU.mult)
                last.then_inc(xn_ready, 1)
            for g in range(NG):
                v.wait_ge(hw_done, g + 1)
                b = 4 + 2 * (g % 2)
                src = ps[:, b:b + 2, :].rearrange("p b (h c) -> p (b h) c", h=2)
                nc.vector.tensor_copy(hw[:, g * GRP:(g + 1) * GRP, :], src[:, :, 0:F])
                nc.vector.tensor_copy(uv[:, g * GRP:(g + 1) * GRP, :], src[:, :, F:F + 2]).then_inc(hw_copied, 1)
            v.wait_ge(hw_copied, NG)

            m = [0]

            def glink(ins, i, K, j):
                ins.then_inc(g_dve, 1)
                v.wait_ge(g_dve, m[0] + i * K + j)

            def broadcast(src, r):
                with v.Fori(0, T) as i:
                    glink(nc.vector.tensor_copy(part[:, 0:2], src[:, bass.ds(i, 1), :].rearrange("p a c -> p (a c)")), i, 2, 1)
                    for c in range(2):
                        d = nc.vector.tensor_scalar(diag[:, c, :], ident[:, :], part[:, c:c + 1], None, ALU.mult)
                    d.then_inc(g_diag, 1)
                    v.wait_ge(g_bc, i + 1 + r * T)
                    glink(nc.vector.tensor_copy(bcast[:, :, bass.ds(i * P, P)], ps[:, 0:2, 0:P]), i, 2, 2)
                m[0] += 2 * T

            broadcast(uv, 0)
            nc.vector.memset(part[:, :], 0.0).then_inc(g_rowused, 1)
            with v.Fori(0, T) as i:
                v.wait_ge(g_row, i * 16 + 16)
                for k, (cmp, c) in enumerate(((ALU.is_gt, 0), (ALU.is_lt, 1), (ALU.is_lt, 0), (ALU.is_gt, 1))):
                    last = nc.vector.scalar_tensor_tensor(t1[:, :], row[:, :], 0.0, bcast[:, c, :], cmp, ALU.mult,
                                                          accum_out=part[:, k:k + 1])
                    if k < 3:
                        glink(last, i, 5, k + 1)
                last.then_inc(g_rowused, 1)
                v.wait_ge(g_rowused, i + 2)
                glink(nc.vector.tensor_reduce(stat[:, 0:2], part[:, :].rearrange("p (s k) -> p s k", k=2), AX.X, ALU.add), i, 5, 4)
                glink(nc.vector.scalar_tensor_tensor(e_raw[:, bass.ds(i, 1), :].rearrange("p a c -> p (a c)"), stat[:, 0:2], ALPHA,
                                                     stat[:, 0:2], ALU.mult, ALU.max), i, 5, 5)
            m[0] += 5 * T
            glink(nc.vector.tensor_scalar(e_sc[:, :, :], e_raw[:, :, :], 1.0 / BIG, None, ALU.mult), 0, 0, 1)
            m[0] += 1
            broadcast(e_sc, 1)
            with v.Fori(0, T) as i:
                v.wait_ge(g_row, i * 16 + 16 + 16 * T)
                nc.vector.scalar_tensor_tensor(t1[:, :], row[:, :], 0.0, bcast[:, 0, :], ALU.is_le, ALU.subtract)
                glink(nc.vector.scalar_tensor_tensor(t2[:, :], row[:, :], 0.0, bcast[:, 1, :], ALU.is_ge, ALU.subtract), i, 5, 1)
                glink(nc.vector.tensor_tensor(t1[:, :], t1[:, :], t2[:, :], ALU.min), i, 5, 2)
                glink(nc.vector.tensor_reduce(stat[:, 0:1], t1[:, :], AX.X, ALU.min), i, 5, 3)
                nc.vector.tensor_scalar(stat[:, 1:2], stat[:, 0:1], BIG, None, ALU.mult).then_inc(g_t, 1)
                v.wait_ge(g_p, i + 1)
                nc.vector.tensor_tensor(t2[:, :], prob[:, :], row[:, :], ALU.mult).then_inc(g_q, 1)
                v.wait_ge(g_q, i + 1)
                glink(nc.vector.reciprocal(stat[:, 3:4], stat[:, 2:3]), i, 5, 4)
                glink(nc.vector.tensor_copy(part[:, 0:1], stat[:, 3:4]), i, 5, 5)
                nc.vector.memset(part[:, 1:2], 0.0).then_inc(g_rowused, 1)
                v.wait_ge(g_prod, i + 1)
                nc.vector.scalar_tensor_tensor(out_t[:, :], ps[:, 5, 0:F], stat[:, 3:4],
                                               x_sb[:, bass.ds(i, 1), :].rearrange("p a f -> p (a f)"),
                                               ALU.mult, ALU.add).then_inc(g_out, 1)
                v.wait_ge(g_stored, i * 16 + 16)


_INS = ['x', 'adj', 'L0_gnn_W', 'L0_gnn_a']


def kernel(**inputs):
    import concourse.bacc as bacc
    from concourse.bass_utils import run_bass_kernel_spmd as run

    nc = bacc.Bacc("TRN2", target_bir_lowering=False, num_devices=1)
    arrays, args = {}, []
    for name in _INS:
        arr = np.ascontiguousarray(inputs[name])
        arrays[f"in_{name}"] = arr
        args.append(nc.dram_tensor(f"in_{name}", arr.shape, mybir.dt.from_np(arr.dtype), kind="ExternalInput").ap())
    out = nc.dram_tensor("out_0", inputs["x"].shape, mybir.dt.float32, kind="ExternalOutput").ap()
    build(nc, *args, out)
    res = run(nc, [arrays], core_ids=[0])
    return res.results[0]["out_0"]
```

```python
import numpy as np
import concourse.bass as bass
from concourse import mybir
from contextlib import ExitStack

P = 128
FP32 = mybir.dt.float32
FP32R = mybir.dt.float32r
BF16 = mybir.dt.bfloat16
INT32 = mybir.dt.int32
ALU = mybir.AluOpType
ACT = mybir.ActivationFunctionType
AX = mybir.AxisListType

EPS = 1e-5
ALPHA = 0.2
Z_LOW, Z_HIGH = 1e-18, 1e30
SCORE_HIGH = 70.0
CB = 8
F_COLS, U_COLS, ONE_COL, N_COLS = slice(0, 3), slice(3, 6), 6, 7


class Group:

    def __init__(self, phase, q0, pairs, low, blocks):
        self.phase, self.q0, self.pairs, self.low = phase, q0, pairs, low
        self.first = 0 if phase == 1 else low // CB
        self.C = blocks // CB - self.first
        self.gaps = {}
        self.positions = [(h, self.first + c) for h in range(2) for c in range(self.C)]

    def product(self, c):
        return self.phase == 2 or c < self.low // CB

    def transposed_slot(self, pos):
        return pos % 3

    def evacuated_slot(self, pos):
        return pos % {4: 4, 3: 3, 2: 4, 1: 2}[self.C]

    def act_masks(self):
        if self.phase == 1:
            return [p for p, (h, c) in enumerate(self.positions) if self.product(c)]
        return [p for p in range(2 * self.C) if p % 2 == 0]


def schedule(T):
    blocks = T
    bounds = [(0, 5, 0), (5, 4, 8), (9, 4, 16), (13, 3, 24)]
    groups = [Group(phase, q0, pairs, low, blocks) for phase in (1, 2) for q0, pairs, low in bounds]
    n = tile = masks = pair = 0
    loads = [0] * (2 * blocks // CB)
    for g in groups:
        g.n0, g.tile0, g.masks0, g.pair0, g.loads0 = n, tile, masks, pair, list(loads)
        n += g.pairs * 2 * g.C
        tile += 2 * g.pairs
        masks += g.pairs * len(g.act_masks())
        pair += g.pairs
        for s in range(2 * g.C):
            loads[s] += g.pairs
    for name, slot_of, far in (("load_gap", lambda g, p: p, 8), ("transposed_gap", Group.transposed_slot, 3),
                               ("evacuated_gap", Group.evacuated_slot, 4)):
        last = {}
        for g in groups:
            gaps = [far] * (2 * g.C)
            for i in range(g.pairs):
                for p in range(2 * g.C):
                    n = g.n0 + i * 2 * g.C + p
                    s = slot_of(g, p)
                    if s in last:
                        gaps[p] = min(gaps[p], n - last[s])
                    last[s] = n
            g.gaps[name] = gaps
    return groups


def shared_tensors(nc, ctx, T, F):
    def sb(name, shape, dt=FP32):
        return ctx.enter_context(nc.sbuf_tensor(name, shape, dt))

    class S:
        x_sb = sb("x_sb", [P, T, F])
        hw = sb("hw", [P, T, F])
        uv = sb("uv", [P, T, 2])
        ident = sb("ident", [P, P])
        ones = sb("ones", [P, P])
        flag = sb("flag", [P, 1], INT32)
    return S


def main_path(nc, S, x, adj, W, a, out):
    N, F = x.shape
    T = N // P
    CW = CB * P
    GRP = 4
    NG = T // GRP
    XG = 8
    groups = schedule(T)

    x_rows = x.rearrange("(t p) f -> p t f", p=P)
    out_rows = out.rearrange("(t p) f -> p t f", p=P)
    adj_rows = adj.rearrange("(t p) n -> p t n", p=P)
    x_sb, hw, uv, ident, ones = S.x_sb, S.hw, S.uv, S.ident, S.ones

    with ExitStack() as ctx:
        def sb(name, shape, dt=FP32):
            return ctx.enter_context(nc.sbuf_tensor(name, shape, dt))

        def sem(name):
            return ctx.enter_context(nc.semaphore(name))

        W_aug = sb("W_aug", [P, F + 2])
        W_T = sb("W_T", [P, F])
        a_sb = sb("a_sb", [P, 2])
        stats = sb("stats", [P, T, 6])
        mv = sb("mv", [P, T, 2])
        var_eps = sb("var_eps", [P, T])
        std = sb("std", [P, T])
        rstd0 = sb("rstd0", [P, T])
        newton = sb("newton", [P, T])
        rstd = sb("rstd", [P, T])
        hT = sb("hT", [P, 2, GRP * P])
        u_rest = sb("u_rest", [P, 2, T])
        loaded_rows = sb("loaded_rows", [P, 2 * T // CB, CW])
        high = sb("high", [P, 4, CW], FP32R)
        low = sb("low", [P, 4, CW], FP32R)
        mask = sb("mask", [P, 4, CW], BF16)
        scratch = sb("scratch", [P, 2, CW], BF16)
        G_high = sb("G_high", [P, T, F], FP32R)
        G_low = sb("G_low", [P, T, F], FP32R)
        cols = sb("cols", [P, T, N_COLS + 1], BF16)
        G_pair = sb("G_pair", [P, 2, F])
        f_pair = sb("f_pair", [P, 2])
        f_rest = sb("f_rest", [P, 2, 2])
        f_parts = sb("f_parts", [P, 2, 3], BF16)
        acc = sb("acc", [P, T, F])
        sums = sb("sums", [P, T, N_COLS + 1])
        e_plus = sb("e_plus", [P, T])
        Z = sb("Z", [P, T])
        joined = sb("joined", [P, 2, F])
        small = sb("small", [P, 8])
        least = sb("least", [P, 2 * T // CB])
        least_loaded = sb("least_loaded", [P, 2 * T // CB])
        shift = sb("shift", [P, 1])
        scores = sb("scores", [P, 2])
        check = sb("check", [P, 4, T])
        verdict = sb("verdict", [P, 4])

        ps = ctx.enter_context(nc.psum_tensor("ps", [P, 8, 512], FP32))

        x_loaded = [sem(f"x_loaded{g}") for g in range(T // XG)]
        w_loaded = sem("w_loaded")
        ident_zero = sem("ident_zero")
        const_ready = sem("const_ready")
        wT_done = sem("wT_done")
        wT_copied = sem("wT_copied")
        wa_done = sem("wa_done")
        wa_copied = sem("wa_copied")
        var_ready = sem("var_ready")
        std_ready = sem("std_ready")
        xn_ready = sem("xn_ready")
        hT_done = sem("hT_done")
        hT_copied = sem("hT_copied")
        hw_done = sem("hw_done")
        hw_copied = sem("hw_copied")
        u_ready = sem("u_ready")
        dve_step = sem("dve_step")
        pool_step = sem("pool_step")
        chunk_loaded = [sem(f"chunk_loaded{s}") for s in range(2 * T // CB)]
        transposed = sem("transposed")
        first_read = sem("first_read")
        act_masked = sem("act_masked")
        evacuated = sem("evacuated")
        multiplied = sem("multiplied")
        tile_posted = sem("tile_posted")
        shift_ready = sem("shift_ready")
        scores_ready = sem("scores_ready")
        f_ready = sem("f_ready")
        G_high_ready = sem("G_high_ready")
        G_pair_ready = sem("G_pair_ready")
        cols_ready = sem("cols_ready")
        G_ready = sem("G_ready")
        row_bad = sem("row_bad")
        all_bad = sem("all_bad")
        stored = sem("stored")
        FREE_LOADED, FREE_EVACUATED, FREE_SUMS, FREE_PAIR = 8, 4, 2, 1

        block = ctx.enter_context(nc.Block())

        def pair_loop(engine, g, body, start=0):
            if g.pairs - start == 1:
                body(start)
            elif g.pairs > start:
                with engine.Fori(start, g.pairs) as i:
                    body(i)

        @block.sync
        def _(sp):
            for k in range(T // XG):
                sp.dma_start(x_sb[:, k * XG:(k + 1) * XG, :],
                             x_rows[:, k * XG:(k + 1) * XG, :]).then_inc(x_loaded[k], 16)
            for g in groups:
                def body(i):
                    for pos, (h, c) in enumerate(g.positions):
                        n = g.n0 + i * 2 * g.C + pos
                        sp.wait_ge(evacuated, n - g.gaps["load_gap"][pos] + 1 + FREE_LOADED)
                        sp.dma_start(loaded_rows[:, pos, :].rearrange("p (a n) -> p a n", a=1),
                                     adj_rows[:, bass.ds((g.q0 + i) * 2 + h, 1), c * CW:(c + 1) * CW])\
                            .then_inc(chunk_loaded[pos], 16)
                pair_loop(sp, g, body)

        @block.gpsimd
        def _(pool):
            nc.gpsimd.memset(ident[:, :], 0.0).then_inc(ident_zero, 1)
            nc.gpsimd.memset(ones[:, :], 1.0).then_inc(const_ready, 1)
            pool.wait_ge(ident_zero, 1)
            nc.gpsimd.affine_select(out=ident[:, :], in_=ident[:, :], compare_op=ALU.not_equal, fill=1.0,
                                    base=0, pattern=[[-1, P]], channel_multiplier=1).then_inc(const_ready, 1)
            pool.wait_ge(tile_posted, 1 + FREE_SUMS)
            nc.gpsimd.partition_all_reduce(shift[:, 0:1], e_plus[:, 0:1], P, bass.bass_isa.ReduceOp.max)\
                .then_inc(shift_ready, 1)
            nc.gpsimd.memset(f_rest[:, :, :], 0.0).then_inc(cols_ready, FREE_PAIR)
            with pool.Fori(0, T // 2) as q:
                steps = 5 * q
                pool.wait_ge(f_ready, q + 1)
                pool.wait_ge(G_ready, q + FREE_PAIR)
                nc.gpsimd.tensor_tensor(G_pair[:, :, :], hw[:, bass.ds(q * 2, 2), :],
                                        f_pair[:, :].unsqueeze(2).to_broadcast([P, 2, F]), ALU.mult)\
                    .then_inc(G_pair_ready, 1)
                rest = f_pair[:, :]
                for k in range(3):
                    nc.gpsimd.tensor_tensor(f_parts[:, :, k], rest, ones[:, 0:2], ALU.mult).then_inc(pool_step, 1)
                    pool.wait_ge(pool_step, steps + 2 * k + 1)
                    if k < 2:
                        nc.gpsimd.tensor_tensor(f_rest[:, k, :], rest, f_parts[:, :, k], ALU.subtract)\
                            .then_inc(pool_step, 1)
                        pool.wait_ge(pool_step, steps + 2 * k + 2)
                        rest = f_rest[:, k, :]
                nc.gpsimd.tensor_copy(cols[:, bass.ds(q * 2, 2), F_COLS], f_parts[:, :, :]).then_inc(cols_ready, 1)
            pool.wait_ge(row_bad, 1)
            nc.gpsimd.partition_all_reduce(verdict[:, 3:4], verdict[:, 2:3], P, bass.bass_isa.ReduceOp.max)\
                .then_inc(all_bad, 1)

        @block.scalar
        def _(act):
            act.dma_start(W_aug[:, 0:F], W[:, :]).then_inc(w_loaded, 16)
            for c in range(2):
                act.dma_start(a_sb[:, c:c + 1], a[c * F:(c + 1) * F, :]).then_inc(w_loaded, 16)
            act.wait_ge(wT_done, 1)
            nc.scalar.activation(W_T[:, :], ps[:, 0, 0:F], ACT.Copy).then_inc(wT_copied, 1)
            act.wait_ge(wa_done, 1)
            nc.scalar.activation(W_aug[:, F:F + 2], ps[:, 1, 0:2], ACT.Copy).then_inc(wa_copied, 1)
            act.wait_ge(var_ready, 1)
            nc.scalar.activation(std[:, :], var_eps[:, :], ACT.Sqrt).then_inc(std_ready, 1)
            for g in range(NG):
                act.wait_ge(hT_done, g + 1)
                if g >= 2:
                    act.wait_ge(hw_done, g - 1)
                nc.scalar.activation(hT[:, g % 2, :], ps[:, 2 + g % 2, :], ACT.Relu).then_inc(hT_copied, 1)

            def pair(g, i, prev):
                for pos, (h, c) in enumerate(g.positions):
                    n = g.n0 + i * 2 * g.C + pos
                    t = g.transposed_slot(pos)
                    s = g.evacuated_slot(pos)
                    src = ps[:, 2 * t:2 * t + 2, :].rearrange("p b n -> p (b n)")
                    act.wait_ge(transposed, n + 1)
                    act.wait_ge(multiplied, n - g.gaps["evacuated_gap"][pos] + 1 + FREE_EVACUATED)
                    if not g.product(c):
                        nc.scalar.activation(mask[:, s, :], src, ACT.Sign).then_inc(first_read, 1)
                    else:
                        nc.scalar.activation(high[:, s, :], src, ACT.Copy).then_inc(first_read, 1)
                        if pos in g.act_masks():
                            act.wait_ge(first_read, n + 1)
                            nc.scalar.activation(mask[:, s, :], high[:, s, :].bitcast(FP32), ACT.Sign)\
                                .then_inc(act_masked, 1)
                    if pos == 2 and prev is not None and prev.phase == 1:
                        q = g.pair0 + i - 1
                        act.wait_ge(scores_ready, q + 1)
                        act.wait_ge(cols_ready, q + FREE_PAIR)
                        nc.scalar.activation(f_pair[:, :], scores[:, :], ACT.Exp).then_inc(f_ready, 1)
                        act.wait_ge(f_ready, q + 1)
                        for k in range(2):
                            done = nc.scalar.activation(G_high[:, bass.ds(q * 2 + k, 1), :],
                                                        hw[:, bass.ds(q * 2 + k, 1), :], ACT.Copy,
                                                        scale=f_pair[:, k:k + 1])
                        done.then_inc(G_high_ready, 1)
                    if pos == min(2, 2 * g.C - 1) and prev is not None and prev.phase == 2:
                        store(g.pair0 + i - 1)

            def store(q):
                act.wait_ge(tile_posted, 2 * q + 2 + FREE_SUMS)
                t = 2 * q - T
                act.dma_start(out_rows[:, bass.ds(t, 2), :], acc[:, bass.ds(t, 2), :]).then_inc(stored, 16)

            prev = None
            for g in groups:
                pair(g, 0, prev)
                pair_loop(act, g, lambda i: pair(g, i, g), start=1)
                prev = g
            store(T - 1)
            act.wait_ge(stored, 16 * (T // 2))

        @block.tensor
        def _(pe):
            pe.wait_ge(const_ready, 2)
            pe.wait_ge(w_loaded, 48)
            nc.tensor.transpose(ps[:, 0, 0:F], W_aug[:, 0:F], ident[:, :]).then_inc(wT_done, 1)
            pe.wait_ge(wT_copied, 1)
            nc.tensor.matmul(ps[:, 1, 0:2], W_T[:, :], a_sb[:, :], start=True, stop=True).then_inc(wa_done, 1)
            pe.wait_ge(wa_copied, 1)

            def project(g):
                pe.wait_ge(hT_copied, g + 1)
                if g >= 2:
                    pe.wait_ge(hw_copied, g - 1)
                for k in range(GRP):
                    b = 4 + 2 * (g % 2) + k // 2
                    o = 256 * (k % 2)
                    mm = nc.tensor.matmul(ps[:, b, o:o + F + 2], hT[:, g % 2, k * P:(k + 1) * P], W_aug[:, :],
                                          start=True, stop=True)
                mm.then_inc(hw_done, 1)

            for g in range(NG):
                pe.wait_ge(xn_ready, g + 1)
                if g >= 2:
                    pe.wait_ge(hT_copied, g - 1)
                for k in range(GRP):
                    tr = nc.tensor.transpose(ps[:, 2 + g % 2, k * P:(k + 1) * P], acc[:, g * GRP + k, :], ident[:, :])
                tr.then_inc(hT_done, 1)
                if g >= 1:
                    project(g - 1)
            project(NG - 1)
            pe.wait_ge(hw_copied, NG)
            pe.wait_ge(u_ready, 1)

            def transpose_chunk(n, pos, slot, gap, loads):
                pe.wait_ge(chunk_loaded[pos], 16 * loads)
                pe.wait_ge(evacuated, n - gap + 1 + FREE_LOADED)
                for k in range(CB):
                    tr = nc.tensor.transpose(ps[:, 2 * slot + k // 4, (k % 4) * P:(k % 4 + 1) * P],
                                             loaded_rows[:, pos, k * P:(k + 1) * P], ident[:, :])
                tr.then_inc(transposed, 1)

            def multiply_chunk(g, i, pos):
                h, c = g.positions[pos]
                n = g.n0 + i * 2 * g.C + pos
                s = g.evacuated_slot(pos)
                first, last = c == g.first, pos in (g.C - 1, 2 * g.C - 1)
                if first:
                    pe.wait_ge(tile_posted, g.tile0 + 2 * i + h + 1)
                if not g.product(c):
                    pe.wait_ge(first_read, n + 1)
                else:
                    pe.wait_ge(evacuated, n + 1 + FREE_LOADED)
                    if pos in g.act_masks():
                        k = g.act_masks().index(pos)
                        pe.wait_ge(act_masked, g.masks0 + i * len(g.act_masks()) + k + 1)
                    pe.wait_ge(G_ready, CB // 2 * (c + 1) + FREE_PAIR)
                    pe.wait_ge(cols_ready, CB // 2 * (c + 1) + FREE_PAIR)
                parts = []
                if g.product(c):
                    for k in range(CB):
                        for left, right in ((high, G_high), (high, G_low), (low, G_high)):
                            parts.append((ps[:, 6 + h, 0:F], left[:, s, k * P:(k + 1) * P], right[:, c * CB + k, :]))
                if g.phase == 2:
                    used = F_COLS
                else:
                    used = slice(0 if g.product(c) else U_COLS.start, N_COLS)
                for k in range(CB):
                    parts.append((ps[:, 6 + h, F + used.start:F + used.stop], mask[:, s, k * P:(k + 1) * P],
                                  cols[:, c * CB + k, used]))
                for j, (sums_out, left, right) in enumerate(parts):
                    mm = nc.tensor.matmul(sums_out, left, right, start=first and j == 0,
                                          stop=last and j == len(parts) - 1, skip_group_check=True)
                mm.then_inc(multiplied, 1)

            multiplied_start = nc.tensor.matmul(ps[:, 0, 0:1], ident[:, :], ident[:, 0:1], start=True, stop=True)
            multiplied_start.then_inc(multiplied, FREE_EVACUATED)
            g = groups[0]
            for pos in range(2):
                transpose_chunk(pos, pos, pos, g.gaps["transposed_gap"][pos], 1)
            for k, g in enumerate(groups):
                after = groups[k + 1] if k + 1 < len(groups) else g
                width = 2 * g.C

                def body(i, ahead=True):
                    for pos in range(width):
                        p = pos + 2
                        if p < width:
                            transpose_chunk(g.n0 + i * width + p, p, g.transposed_slot(p), g.gaps["transposed_gap"][p],
                                            g.loads0[p] + i + 1)
                        elif ahead:
                            p -= width
                            transpose_chunk(g.n0 + (i + 1) * width + p, p, g.transposed_slot(p),
                                            min(g.gaps["transposed_gap"][p], after.gaps["transposed_gap"][p]), g.loads0[p] + i + 2)
                        multiply_chunk(g, i, pos)
                if k + 1 < len(groups):
                    pair_loop(pe, g, body)
                else:
                    with pe.Fori(0, g.pairs - 1) as i:
                        body(i)
                    body(g.pairs - 1, ahead=False)

        @block.vector
        def _(v):
            steps = [0]

            def link(ins, step=None):
                if step is None:
                    steps[0] += 1
                    step = steps[0]
                ins.then_inc(dve_step, 1)
                v.wait_ge(dve_step, step)

            nc.vector.memset(least[:, :], 0.0).then_inc(evacuated, FREE_LOADED)
            nc.vector.memset(least_loaded[:, :], 0.0)
            nc.vector.memset(cols[:, :, ONE_COL], 1.0)
            for g in range(T // XG):
                v.wait_ge(x_loaded[g], 16)
                for t in range(g * XG, (g + 1) * XG):
                    last = nc.vector.bn_stats(stats[:, t, :], x_sb[:, t, :])
            link(last)
            for t in range(T):
                last = nc.vector.bn_aggr(mv[:, t, :], stats[:, t, :])
            link(last)
            nc.vector.tensor_scalar(var_eps[:, :], mv[:, :, 1], EPS, None, ALU.add).then_inc(var_ready, 1)
            v.wait_ge(std_ready, 1)
            link(nc.vector.reciprocal(rstd0[:, :], std[:, :]))
            link(nc.vector.tensor_tensor(newton[:, :], rstd0[:, :], rstd0[:, :], ALU.mult))
            link(nc.vector.tensor_tensor(newton[:, :], newton[:, :], var_eps[:, :], ALU.mult))
            link(nc.vector.tensor_scalar(newton[:, :], newton[:, :], -0.5, 1.5, ALU.mult, ALU.add))
            link(nc.vector.tensor_tensor(rstd[:, :], rstd0[:, :], newton[:, :], ALU.mult))
            for g in range(NG):
                for t in range(g * GRP, (g + 1) * GRP):
                    last = nc.vector.tensor_scalar(acc[:, t, :], x_sb[:, t, :], mv[:, t, 0:1], rstd[:, t:t + 1],
                                                   ALU.subtract, ALU.mult)
                last.then_inc(xn_ready, 1)
            for g in range(NG):
                v.wait_ge(hw_done, g + 1)
                b = 4 + 2 * (g % 2)
                src = ps[:, b:b + 2, :].rearrange("p b (h c) -> p (b h) c", h=2)
                nc.vector.tensor_copy(hw[:, g * GRP:(g + 1) * GRP, :], src[:, :, 0:F])
                nc.vector.tensor_copy(uv[:, g * GRP:(g + 1) * GRP, :], src[:, :, F:F + 2]).then_inc(hw_copied, 1)
            v.wait_ge(hw_copied, NG)
            rest = uv[:, :, 0]
            for k in range(3):
                part = cols[:, :, U_COLS.start + k]
                copied = nc.vector.tensor_copy(part, rest)
                if k < 2:
                    link(copied)
                    link(nc.vector.tensor_tensor(u_rest[:, k, :], rest, part, ALU.subtract))
                    rest = u_rest[:, k, :]
                else:
                    copied.then_inc(u_ready, 1)
            nc.vector.memset(small[:, 0:1], 0.0).then_inc(tile_posted, FREE_SUMS)
            nc.vector.memset(small[:, 1:2], 0.0).then_inc(G_ready, FREE_PAIR)

            step0 = steps[0]

            def post(g, i, h):
                tile = g.tile0 + 2 * i + h
                bank = 6 + h
                last_chunk = g.n0 + i * 2 * g.C + (h + 1) * g.C
                v.wait_ge(multiplied, last_chunk + FREE_EVACUATED)
                if g.phase == 1:
                    step = step0 + tile
                    t = bass.ds(tile, 1)
                    used = slice(0 if g.low else U_COLS.start, N_COLS)
                    if g.low:
                        nc.vector.tensor_copy(acc[:, t, :], ps[:, bank:bank + 1, 0:F])
                    nc.vector.tensor_copy(sums[:, t, used], ps[:, bank:bank + 1, F + used.start:F + used.stop])
                    link(nc.vector.tensor_reduce(small[:, h:h + 1], ps[:, bank, F + U_COLS.start:F + U_COLS.stop],
                                                 AX.X, ALU.add), step + 1)
                    nc.vector.scalar_tensor_tensor(e_plus[:, t], small[:, h:h + 1], ALPHA, small[:, h:h + 1],
                                                   ALU.mult, ALU.max).then_inc(tile_posted, 1)
                else:
                    row = tile - T
                    step = step0 + T + 4 * row
                    t = bass.ds(row, 1)
                    f_sums = ps[:, bank:bank + 1, F + F_COLS.start:F + F_COLS.stop]
                    parts = small[:, 4:7].unsqueeze(1)
                    if g.low:
                        link(nc.vector.tensor_tensor(parts, f_sums, sums[:, t, F_COLS], ALU.add), step + 1)
                    else:
                        link(nc.vector.tensor_copy(parts, f_sums), step + 1)
                    link(nc.vector.tensor_reduce(Z[:, t], small[:, 4:7], AX.X, ALU.add), step + 2)
                    link(nc.vector.tensor_scalar(small[:, 2:3], Z[:, t], Z_LOW, None, ALU.max), step + 3)
                    source = ps[:, bank:bank + 1, 0:F]
                    if g.low:
                        nc.vector.tensor_tensor(joined[:, h:h + 1, :], source, acc[:, t, :], ALU.add)
                        source = joined[:, h:h + 1, :]
                    link(nc.vector.reciprocal(small[:, 3:4], small[:, 2:3]), step + 4)
                    nc.vector.scalar_tensor_tensor(acc[:, t, :].rearrange("p a f -> p (a f)"),
                                                   source.rearrange("p a f -> p (a f)"), small[:, 3:4],
                                                   x_sb[:, t, :].rearrange("p a f -> p (a f)"),
                                                   ALU.mult, ALU.add).then_inc(tile_posted, 1)

            def relative_scores(q):
                v.wait_ge(tile_posted, 2 * q + 2 + FREE_SUMS)
                v.wait_ge(shift_ready, 1)
                v.wait_ge(G_ready, q + FREE_PAIR)
                nc.vector.tensor_scalar(scores[:, :], e_plus[:, bass.ds(q * 2, 2)], shift[:, 0:1], SCORE_HIGH,
                                        ALU.subtract, ALU.min).then_inc(scores_ready, 1)

            def pair(g, i, prev):
                for pos, (h, c) in enumerate(g.positions):
                    n = g.n0 + i * 2 * g.C + pos
                    t = g.transposed_slot(pos)
                    s = g.evacuated_slot(pos)
                    src = ps[:, 2 * t:2 * t + 2, :].rearrange("p b n -> p (b n)")
                    v.wait_ge(first_read, n + 1)
                    if not g.product(c):
                        v.wait_ge(evacuated, n + FREE_LOADED - 1)
                        nc.vector.tensor_scalar(scratch[:, pos % 2, :], src, 1.0, least[:, pos:pos + 1], ALU.mult, ALU.min,
                                                accum_out=least[:, pos:pos + 1]).then_inc(evacuated, 1)
                    else:
                        if g.phase == 1:
                            v.wait_ge(evacuated, n + FREE_LOADED - 1)
                            nc.vector.tensor_scalar(scratch[:, pos % 2, :], loaded_rows[:, pos, :], 1.0,
                                                    least_loaded[:, pos:pos + 1], ALU.mult, ALU.min,
                                                    accum_out=least_loaded[:, pos:pos + 1])
                        elif pos not in g.act_masks():
                            nc.vector.tensor_scalar(mask[:, s, :], high[:, s, :].bitcast(FP32), 0.0, None, ALU.is_gt)
                        nc.vector.tensor_tensor(low[:, s, :], src, high[:, s, :].bitcast(FP32), ALU.subtract)\
                            .then_inc(evacuated, 1)
                    if pos == 0 and prev is not None:
                        post_of(prev, g, i)
                        if prev.phase == 1:
                            relative_scores(g.pair0 + i - 1)
                    if pos == 4 and prev is not None and prev.phase == 1:
                        q = g.pair0 + i - 1
                        v.wait_ge(G_pair_ready, q + 1)
                        v.wait_ge(G_high_ready, q + 1)
                        nc.vector.tensor_tensor(G_low[:, bass.ds(q * 2, 2), :], G_pair[:, :, :],
                                                G_high[:, bass.ds(q * 2, 2), :].bitcast(FP32),
                                                ALU.subtract).then_inc(G_ready, 1)
                    if pos == g.C:
                        post(g, i, 0)

            def post_of(prev, g, i):
                if prev is g:
                    post(g, i - 1, 1)
                else:
                    post(prev, prev.pairs - 1, 1)


            prev = None
            for g in groups:
                pair(g, 0, prev)
                pair_loop(v, g, lambda i: pair(g, i, g), start=1)
                prev = g
            post(g, g.pairs - 1, 1)
            steps[0] = step0 + T + 4 * T
            everything = least_loaded[:, :]
            nc.vector.tensor_tensor(everything, least[:, :], least_loaded[:, :], ALU.min)
            link(nc.vector.tensor_scalar(check[:, 0, :], Z[:, :], Z_LOW, None, ALU.is_ge))
            nc.vector.tensor_scalar(check[:, 1, :], Z[:, :], Z_HIGH, None, ALU.is_le)
            nc.vector.tensor_scalar(check[:, 2, :], sums[:, :, ONE_COL], 0.0, None, ALU.is_gt)
            link(nc.vector.tensor_reduce(verdict[:, 0:1], everything, AX.X, ALU.min))
            nc.vector.tensor_scalar(verdict[:, 1:2], verdict[:, 0:1], 0.0, None, ALU.is_lt)
            link(nc.vector.tensor_tensor(check[:, 3, :], check[:, 0, :], check[:, 1, :], ALU.mult))
            link(nc.vector.tensor_tensor(check[:, 0, :], check[:, 2, :], check[:, 3, :], ALU.is_gt))
            link(nc.vector.tensor_reduce(verdict[:, 0:1], check[:, 0, :], AX.X, ALU.max))
            nc.vector.tensor_tensor(verdict[:, 2:3], verdict[:, 0:1], verdict[:, 1:2], ALU.max).then_inc(row_bad, 1)
            v.wait_ge(all_bad, 1)
            link(nc.vector.tensor_copy(S.flag[:, :], verdict[:, 3:4]))


def general_path(nc, S, adj, out):
    N = adj.shape[0]
    T, F = S.hw.shape[1], S.hw.shape[2]
    BIG = 2.0 ** 53
    GRP = 4
    NG = T // GRP
    hw, uv, x_sb, ident, ones = S.hw, S.uv, S.x_sb, S.ident, S.ones
    out_rows = out.rearrange("(t p) f -> p t f", p=P)
    adj_rows = adj.rearrange("(t p) n -> p t n", p=P)

    with ExitStack() as ctx:
        def sb(name, shape, dt=FP32):
            return ctx.enter_context(nc.sbuf_tensor(name, shape, dt))

        def sem(name):
            return ctx.enter_context(nc.semaphore(name))

        bcast = sb("bcast", [P, 2, N])
        row = sb("row", [P, N])
        t1 = sb("t1", [P, N])
        t2 = sb("t2", [P, N])
        prob = sb("prob", [P, N])
        probT = sb("probT", [P, N])
        diag = sb("diag", [P, 2, P])
        part = sb("part", [P, 4])
        e_raw = sb("e_raw", [P, T, 2])
        e_sc = sb("e_sc", [P, T, 2])
        stat = sb("stat", [P, 4])
        out_t = sb("out_t", [P, F])
        gps = ctx.enter_context(nc.psum_tensor("gps", [P, 8, 512], FP32))
        g_diag = sem("g_diag")
        g_bc = sem("g_bc")
        g_bcc = sem("g_bcc")
        g_row = sem("g_row")
        g_rowused = sem("g_rowused")
        g_dve = sem("g_dve")
        g_t = sem("g_t")
        g_p = sem("g_p")
        g_q = sem("g_q")
        g_qT = sem("g_qT")
        g_qTc = sem("g_qTc")
        g_prod = sem("g_prod")
        g_out = sem("g_out")
        g_stored = sem("g_stored")
        block = ctx.enter_context(nc.Block())

        def flagged(engine):
            return engine.value_load(S.flag[0:1, 0:1], min_val=0, max_val=1)

        @block.sync
        def _(sp):
            with sp.If(flagged(sp)):
                with sp.Fori(0, T) as i:
                    sp.wait_ge(g_rowused, i + 1)
                    sp.dma_start(row[:, :], adj_rows[:, bass.ds(i, 1), :].rearrange("p a n -> p (a n)")).then_inc(g_row, 16)
                with sp.Fori(0, T) as i:
                    sp.wait_ge(g_rowused, i + 1 + T)
                    sp.dma_start(row[:, :], adj_rows[:, bass.ds(i, 1), :].rearrange("p a n -> p (a n)")).then_inc(g_row, 16)
                    sp.wait_ge(g_out, i + 1)
                    sp.dma_start(out_rows[:, bass.ds(i, 1), :], out_t[:, :].rearrange("p (a f) -> p a f", a=1)).then_inc(g_stored, 16)
                sp.wait_ge(g_stored, 16 * T)

        @block.scalar
        def _(act):
            with act.If(flagged(act)):
                with act.Fori(0, T) as i:
                    act.wait_ge(g_t, i + 1)
                    nc.scalar.activation(prob[:, :], t1[:, :], ACT.Exp, bias=stat[:, 1:2], scale=-BIG,
                                         accum_out=stat[:, 2:3]).then_inc(g_p, 1)
                    for g in range(NG):
                        act.wait_ge(g_qT, i * NG + g + 1)
                        nc.scalar.activation(probT[:, g * 512:(g + 1) * 512], gps[:, g % 4, :],
                                             ACT.Copy).then_inc(g_qTc, 1)

        @block.tensor
        def _(pe):
            with pe.If(flagged(pe)):
                for r in range(2):
                    with pe.Fori(0, T) as i:
                        pe.wait_ge(g_diag, i + 1 + r * T)
                        for c in range(2):
                            mm = nc.tensor.matmul(gps[:, c, 0:P], ones[:, :], diag[:, c, :], start=True, stop=True)
                        mm.then_inc(g_bc, 1)
                with pe.Fori(0, T) as i:
                    pe.wait_ge(g_q, i + 1)
                    for g in range(NG):
                        if g >= 4:
                            pe.wait_ge(g_qTc, i * NG + g - 3)
                        for k in range(GRP):
                            b = g * GRP + k
                            tr = nc.tensor.transpose(gps[:, g % 4, k * P:(k + 1) * P], t2[:, b * P:(b + 1) * P], ident[:, :])
                        tr.then_inc(g_qT, 1)
                    pe.wait_ge(g_qTc, i * NG + NG)
                    for b in range(T):
                        mm = nc.tensor.matmul(gps[:, 5, 0:F], probT[:, b * P:(b + 1) * P], hw[:, b, :],
                                              start=b == 0, stop=b == T - 1)
                    mm.then_inc(g_prod, 1)

        @block.vector
        def _(v):
            with v.If(flagged(v)):
                m = [0]

                def glink(ins, i, K, j):
                    ins.then_inc(g_dve, 1)
                    v.wait_ge(g_dve, m[0] + i * K + j)

                def broadcast(src, r):
                    with v.Fori(0, T) as i:
                        glink(nc.vector.tensor_copy(part[:, 0:2], src[:, bass.ds(i, 1), :].rearrange("p a c -> p (a c)")), i, 2, 1)
                        for c in range(2):
                            d = nc.vector.tensor_scalar(diag[:, c, :], ident[:, :], part[:, c:c + 1], None, ALU.mult)
                        d.then_inc(g_diag, 1)
                        v.wait_ge(g_bc, i + 1 + r * T)
                        glink(nc.vector.tensor_copy(bcast[:, :, bass.ds(i * P, P)], gps[:, 0:2, 0:P]), i, 2, 2)
                    m[0] += 2 * T

                broadcast(uv, 0)
                nc.vector.memset(part[:, :], 0.0).then_inc(g_rowused, 1)
                with v.Fori(0, T) as i:
                    v.wait_ge(g_row, i * 16 + 16)
                    for k, (cmp, c) in enumerate(((ALU.is_gt, 0), (ALU.is_lt, 1), (ALU.is_lt, 0), (ALU.is_gt, 1))):
                        last = nc.vector.scalar_tensor_tensor(t1[:, :], row[:, :], 0.0, bcast[:, c, :], cmp, ALU.mult,
                                                              accum_out=part[:, k:k + 1])
                        if k < 3:
                            glink(last, i, 5, k + 1)
                    last.then_inc(g_rowused, 1)
                    v.wait_ge(g_rowused, i + 2)
                    glink(nc.vector.tensor_reduce(stat[:, 0:2], part[:, :].rearrange("p (s k) -> p s k", k=2), AX.X, ALU.add), i, 5, 4)
                    glink(nc.vector.scalar_tensor_tensor(e_raw[:, bass.ds(i, 1), :].rearrange("p a c -> p (a c)"), stat[:, 0:2], ALPHA,
                                                         stat[:, 0:2], ALU.mult, ALU.max), i, 5, 5)
                m[0] += 5 * T
                glink(nc.vector.tensor_scalar(e_sc[:, :, :], e_raw[:, :, :], 1.0 / BIG, None, ALU.mult), 0, 0, 1)
                m[0] += 1
                broadcast(e_sc, 1)
                with v.Fori(0, T) as i:
                    v.wait_ge(g_row, i * 16 + 16 + 16 * T)
                    nc.vector.scalar_tensor_tensor(t1[:, :], row[:, :], 0.0, bcast[:, 0, :], ALU.is_le, ALU.subtract)
                    glink(nc.vector.scalar_tensor_tensor(t2[:, :], row[:, :], 0.0, bcast[:, 1, :], ALU.is_ge, ALU.subtract), i, 5, 1)
                    glink(nc.vector.tensor_tensor(t1[:, :], t1[:, :], t2[:, :], ALU.min), i, 5, 2)
                    glink(nc.vector.tensor_reduce(stat[:, 0:1], t1[:, :], AX.X, ALU.min), i, 5, 3)
                    nc.vector.tensor_scalar(stat[:, 1:2], stat[:, 0:1], BIG, None, ALU.mult).then_inc(g_t, 1)
                    v.wait_ge(g_p, i + 1)
                    nc.vector.tensor_tensor(t2[:, :], prob[:, :], row[:, :], ALU.mult).then_inc(g_q, 1)
                    v.wait_ge(g_q, i + 1)
                    glink(nc.vector.reciprocal(stat[:, 3:4], stat[:, 2:3]), i, 5, 4)
                    glink(nc.vector.tensor_copy(part[:, 0:1], stat[:, 3:4]), i, 5, 5)
                    nc.vector.memset(part[:, 1:2], 0.0).then_inc(g_rowused, 1)
                    v.wait_ge(g_prod, i + 1)
                    nc.vector.scalar_tensor_tensor(out_t[:, :], gps[:, 5, 0:F], stat[:, 3:4],
                                                   x_sb[:, bass.ds(i, 1), :].rearrange("p a f -> p (a f)"),
                                                   ALU.mult, ALU.add).then_inc(g_out, 1)
                    v.wait_ge(g_stored, i * 16 + 16)



def build(nc, x, adj, W, a, out):
    N, F = x.shape
    with ExitStack() as ctx:
        S = shared_tensors(nc, ctx, N // P, F)
        main_path(nc, S, x, adj, W, a, out)
        general_path(nc, S, adj, out)


_INS = ['x', 'adj', 'L0_gnn_W', 'L0_gnn_a']


def kernel(**inputs):
    import concourse.bacc as bacc
    from concourse.bass_utils import run_bass_kernel_spmd as run

    nc = bacc.Bacc("TRN2", target_bir_lowering=False, num_devices=1)
    arrays, args = {}, []
    for name in _INS:
        arr = np.ascontiguousarray(inputs[name])
        arrays[f"in_{name}"] = arr
        args.append(nc.dram_tensor(f"in_{name}", arr.shape, mybir.dt.from_np(arr.dtype), kind="ExternalInput").ap())
    out = nc.dram_tensor("out_0", inputs["x"].shape, mybir.dt.float32, kind="ExternalOutput").ap()
    build(nc, *args, out)
    res = run(nc, [arrays], core_ids=[0])
    return res.results[0]["out_0"]
```

```python
import numpy as np
import concourse.bass as bass
from concourse import mybir
from contextlib import ExitStack

P = 128
FP32 = mybir.dt.float32
FP32R = mybir.dt.float32r
BF16 = mybir.dt.bfloat16
INT32 = mybir.dt.int32
ALU = mybir.AluOpType
ACT = mybir.ActivationFunctionType
AX = mybir.AxisListType

EPS = 1e-5
ALPHA = 0.2
Z_LOW, Z_HIGH = 1e-18, 1e30
SCORE_HIGH = 70.0
QT, CB = 4, 2
SCORES, FINAL = "scores", "final"
LOADED, MASKS, EVACUATED = 12, 4, 4
TRANSPOSED_BANKS, PRODUCT_BANKS, SUMS_BANK = {SCORES: 5, FINAL: 4}, {SCORES: (5, 5), FINAL: (4, 5)}, 6
POST_AFTER, F_AFTER, G_AFTER, OUTPUT_AFTER = 3, 5, 7, 8
AHEAD, MASK_AHEAD = 3, 4
EARLY_MASKED, EARLY_TRANSPOSED, EARLY_EVACUATED = 8, 6, 4
F_COLS, U_COLS, ONE_COL, N_COLS = slice(0, 3), slice(3, 6), 6, 7
MASKED, PRODUCT, OUTPUT = "masked", "product", "output"


class Item:

    def __init__(self, kind, visit, columns=None, pos=None):
        self.kind, self.visit, self.columns, self.pos = kind, visit, columns, pos


class Visit:

    def __init__(self, number, kind, q, known, columns):
        self.number, self.kind, self.q = number, kind, q
        if kind == SCORES:
            newest = max(known - 1, 0)
            masked = [Item(MASKED, self, c) for c in range(known, columns)]
            old = [Item(PRODUCT, self, c) for c in range(newest)]
            places = [(k / len(masked), it) for k, it in enumerate(masked)]
            places += [((k + 0.5) / len(old), it) for k, it in enumerate(old)]
            self.items = [it for _, it in sorted(places, key=lambda e: e[0])]
            self.items += [Item(PRODUCT, self, c) for c in range(newest, known)]
        else:
            self.items = [Item(PRODUCT, self, c) for c in range(known, columns)]
        for pos, it in enumerate(self.items):
            it.pos = pos
        self.chunks = len(self.items)
        self.sums_bank = SUMS_BANK + number % 2
        self.product_bank = PRODUCT_BANKS[kind][number % 2]
        products = [it for it in self.items if it.kind == PRODUCT]
        self.first_product, self.last_product = (products[0], products[-1]) if products else (None, None)


def schedule(T):
    quads, per_quad, columns = T // QT, QT // CB, T // CB
    order = [(SCORES, q) for q in range(quads)]
    order += [(FINAL, quads - (k + 1) // 2 if k % 2 else k // 2) for k in range(quads)]
    visits = [Visit(v, kind, q, q * per_quad, columns) for v, (kind, q) in enumerate(order)]
    items, outputs, chunks = [], [], 0
    for visit in visits:
        for it in visit.items:
            items.append(it)
            chunks += 1
            if outputs and chunks == outputs[0][0]:
                items.append(Item(OUTPUT, outputs.pop(0)[1]))
        visit.chunks_done = chunks
        if visit.kind == FINAL:
            outputs.append((chunks + OUTPUT_AFTER, visit))
    items += [Item(OUTPUT, visit) for _, visit in outputs]
    chunk = mask = product = evacuated = outputs_done = 0
    for n, it in enumerate(items):
        it.n, it.chunk, it.mask, it.product, it.evacuated = n, chunk, mask, product, evacuated
        if it.kind == OUTPUT:
            it.number = outputs_done
            outputs_done += 1
        chunk += it.kind != OUTPUT
        mask += it.kind == MASKED
        product += it.kind == PRODUCT
        evacuated += it.kind != MASKED
    posts, fs, gs = {}, {}, {}
    for visit in visits:
        visit.n = visit.items[-1].n
        posts.setdefault(min(visit.n + POST_AFTER, len(items) - 2), []).append(visit)
        if visit.kind == SCORES:
            fs[visit.n + F_AFTER] = visit
            gs[visit.n + G_AFTER] = visit
    last_user = [None] * 6
    for it in items:
        width = 2 if it.kind == PRODUCT else 1
        starts = range(TRANSPOSED_BANKS[it.visit.kind] + 1 - width)
        if it.n < EARLY_TRANSPOSED:
            starts = (0, 2)
        elif width == 1:
            starts = sorted(starts, key=lambda b: abs(b - 2))

        def since(b):
            return max([last_user[k].n for k in range(b, b + width) if last_user[k]] + [it.n - AHEAD - 1])
        it.bank = min(starts, key=since)
        it.users_before = {last_user[k] for k in range(it.bank, it.bank + width)} - {None}
        for k in range(it.bank, it.bank + width):
            last_user[k] = it
        if it is it.visit.first_product:
            it.visit.user_before = last_user[it.visit.product_bank]
            last_user[it.visit.product_bank] = it.visit
    return visits, items, posts, fs, gs


def shared_tensors(nc, ctx, T, F):
    def sb(name, shape, dt=FP32):
        return ctx.enter_context(nc.sbuf_tensor(name, shape, dt))

    class S:
        x_sb = sb("x_sb", [P, T, F])
        hw = sb("hw", [P, T, F])
        uv = sb("uv", [P, T, 2])
        ident = sb("ident", [P, P])
        ones = sb("ones", [P, P])
        flag = sb("flag", [P, 1], INT32)
    return S


def main_path(nc, S, x, adj, W, a, out):
    N, F = x.shape
    T = N // P
    CW = CB * P
    QW = QT * P
    CHUNK = CB * QW
    GRP = 4
    NG = T // GRP
    XG = 8
    visits, items, posts, fs, gs = schedule(T)
    chunks = [it for it in items if it.kind != OUTPUT]

    x_rows = x.rearrange("(t p) f -> p t f", p=P)
    out_rows = out.rearrange("(t p) f -> p t f", p=P)
    adj_rows = adj.rearrange("(t p) n -> p t n", p=P)
    x_sb, hw, uv, ident, ones = S.x_sb, S.hw, S.uv, S.ident, S.ones

    with ExitStack() as ctx:
        def sb(name, shape, dt=FP32):
            return ctx.enter_context(nc.sbuf_tensor(name, shape, dt))

        def sem(name):
            return ctx.enter_context(nc.semaphore(name))

        W_aug = sb("W_aug", [P, F + 2])
        W_T = sb("W_T", [P, F])
        a_sb = sb("a_sb", [P, 2])
        stats = sb("stats", [P, T, 6])
        mv = sb("mv", [P, T, 2])
        var_eps = sb("var_eps", [P, T])
        std = sb("std", [P, T])
        rstd0 = sb("rstd0", [P, T])
        newton = sb("newton", [P, T])
        rstd = sb("rstd", [P, T])
        mean_rstd = sb("mean_rstd", [P, T])
        hT = sb("hT", [P, 2, GRP * P])
        u_rest = sb("u_rest", [P, 2, T])
        ident_bf = sb("ident_bf", [P, P], BF16)
        loaded_rows = sb("loaded_rows", [P, LOADED, CHUNK])
        row_mask = sb("row_mask", [P, MASKS, CHUNK], BF16)
        high = sb("high", [P, EVACUATED, CHUNK], FP32R)
        low = sb("low", [P, EVACUATED, CHUNK], FP32R)
        mask = sb("mask", [P, EVACUATED, CHUNK], BF16)
        unused = sb("unused", [P, 2, CHUNK], BF16)
        G_high = sb("G_high", [P, T, F], FP32R)
        G_low = sb("G_low", [P, T, F], FP32R)
        cols = sb("cols", [P, T, N_COLS + 1], BF16)
        G_quad = sb("G_quad", [P, QT, F])
        f_quad = sb("f_quad", [P, QT])
        f_rest = sb("f_rest", [P, 2, QT])
        f_parts = sb("f_parts", [P, QT, 3], BF16)
        product_T = sb("product_T", [P, T * P])
        xn = product_T[:, :].rearrange("p (t f) -> p t f", f=F)
        out_rows_sb = sb("out_rows_sb", [P, 2, QT, F])
        sums = sb("sums", [P, T, N_COLS + 1])
        e_plus = sb("e_plus", [P, T])
        Z = sb("Z", [P, T])
        Z_held = sb("Z_held", [P, T])
        Z_inverse = sb("Z_inverse", [P, T])
        small = sb("small", [P, QT])
        least = sb("least", [P, T // QT * T // CB])
        first_max = sb("first_max", [P, 1])
        shift = sb("shift", [P, 1])
        scores = sb("scores", [P, QT])
        check = sb("check", [P, 4, T])
        verdict = sb("verdict", [P, 4])

        ps = ctx.enter_context(nc.psum_tensor("ps", [P, 8, 512], FP32))

        x_loaded = [sem(f"x_loaded{g}") for g in range(T // XG)]
        w_loaded = sem("w_loaded")
        ident_zero = sem("ident_zero")
        const_ready = sem("const_ready")
        wT_done = sem("wT_done")
        wT_copied = sem("wT_copied")
        wa_done = sem("wa_done")
        wa_copied = sem("wa_copied")
        var_ready = sem("var_ready")
        std_ready = sem("std_ready")
        norm_ready = sem("norm_ready")
        xn_ready = [sem(f"xn_ready{g}") for g in range(NG)]
        hT_done = sem("hT_done")
        hT_copied = sem("hT_copied")
        hw_done = sem("hw_done")
        hw_copied = sem("hw_copied")
        u_ready = sem("u_ready")
        dve_step = sem("dve_step")
        pool_step = sem("pool_step")
        chunk_loaded = [sem(f"chunk_loaded{s}") for s in range(LOADED)]
        row_masked = sem("row_masked")
        transposed = sem("transposed")
        first_read = sem("first_read")
        act_masked = sem("act_masked")
        checked = sem("checked")
        evacuated = sem("evacuated")
        multiplied = sem("multiplied")
        visit_posted = sem("visit_posted")
        first_max_ready = sem("first_max_ready")
        shift_ready = sem("shift_ready")
        scores_ready = sem("scores_ready")
        f_ready = sem("f_ready")
        G_high_ready = sem("G_high_ready")
        G_quad_ready = sem("G_quad_ready")
        cols_ready = sem("cols_ready")
        G_ready = sem("G_ready")
        row_bad = sem("row_bad")
        out_ready = sem("out_ready")
        all_bad = sem("all_bad")
        stored = [sem(f"stored{s}") for s in range(2)]

        NORM_DVE, NORM_ACT, NORM_POOL = (0, 2), (1, 3, 4), (5, 6, 7)
        FREE_QUAD = 1

        block = ctx.enter_context(nc.Block())

        @block.sync
        def _(sp):
            for k in range(T // XG):
                sp.dma_start(x_sb[:, k * XG:(k + 1) * XG, :],
                             x_rows[:, k * XG:(k + 1) * XG, :]).then_inc(x_loaded[k], 16)

            def store(it):
                sp.wait_ge(out_ready, it.number + 1)
                rows = slice(it.visit.q * QT, (it.visit.q + 1) * QT)
                sp.dma_start(out_rows[:, rows, :], out_rows_sb[:, it.number % 2, :, :])\
                    .then_inc(stored[it.number % 2], 16)

            outputs = [it for it in items if it.kind == OUTPUT]
            for it in chunks:
                s = it.chunk % LOADED
                while it.chunk >= LOADED and outputs and outputs[0].n < chunks[it.chunk - LOADED].n:
                    store(outputs.pop(0))
                if it.chunk >= LOADED:
                    last = chunks[it.chunk - LOADED]
                    if last.kind == MASKED:
                        sp.wait_ge(row_masked, last.mask + 1)
                    else:
                        sp.wait_ge(transposed, last.n + 1)
                sp.dma_start(loaded_rows[:, s, :].rearrange("p (t n) -> p t n", t=QT),
                             adj_rows[:, it.visit.q * QT:(it.visit.q + 1) * QT,
                                      it.columns * CW:(it.columns + 1) * CW]).then_inc(chunk_loaded[s], 16)
            for it in outputs:
                store(it)
            for s in range(2):
                sp.wait_ge(stored[s], 16 * (T // QT // 2))

        @block.gpsimd
        def _(pool):
            nc.gpsimd.memset(ident[:, :], 0.0).then_inc(ident_zero, 1)
            nc.gpsimd.memset(ones[:, :], 1.0).then_inc(const_ready, 1)
            pool.wait_ge(ident_zero, 1)
            nc.gpsimd.affine_select(out=ident[:, :], in_=ident[:, :], compare_op=ALU.not_equal, fill=1.0,
                                    base=0, pattern=[[-1, P]], channel_multiplier=1).then_inc(const_ready, 1)
            pool.wait_ge(const_ready, 2)
            nc.gpsimd.tensor_copy(ident_bf[:, :], ident[:, :]).then_inc(const_ready, 1)
            pool.wait_ge(norm_ready, 1)
            for g in NORM_POOL:
                for t in range(g * GRP, (g + 1) * GRP):
                    done = nc.gpsimd.tensor_scalar(xn[:, t, :], x_sb[:, t, :], mv[:, t, 0:1], rstd[:, t:t + 1],
                                                   ALU.subtract, ALU.mult)
                done.then_inc(xn_ready[g], 1)
            pool.wait_ge(first_max_ready, 1)
            nc.gpsimd.partition_all_reduce(shift[:, :], first_max[:, :], P, bass.bass_isa.ReduceOp.max)\
                .then_inc(shift_ready, 1)
            nc.gpsimd.memset(f_rest[:, :, :], 0.0).then_inc(G_ready, FREE_QUAD)
            with pool.Fori(0, T // QT) as q:
                steps = 5 * q
                pool.wait_ge(f_ready, q + 1)
                pool.wait_ge(G_ready, q + FREE_QUAD)
                nc.gpsimd.tensor_tensor(G_quad[:, :, :], hw[:, bass.ds(q * QT, QT), :],
                                        f_quad[:, :].unsqueeze(2).to_broadcast([P, QT, F]), ALU.mult)\
                    .then_inc(G_quad_ready, 1)
                rest = f_quad[:, :]
                for k in range(3):
                    nc.gpsimd.tensor_tensor(f_parts[:, :, k], rest, ones[:, 0:QT], ALU.mult).then_inc(pool_step, 1)
                    pool.wait_ge(pool_step, steps + 2 * k + 1)
                    if k < 2:
                        nc.gpsimd.tensor_tensor(f_rest[:, k, :], rest, f_parts[:, :, k], ALU.subtract)\
                            .then_inc(pool_step, 1)
                        pool.wait_ge(pool_step, steps + 2 * k + 2)
                        rest = f_rest[:, k, :]
                nc.gpsimd.tensor_copy(cols[:, bass.ds(q * QT, QT), F_COLS], f_parts[:, :, :]).then_inc(cols_ready, 1)
            pool.wait_ge(row_bad, 1)
            nc.gpsimd.partition_all_reduce(verdict[:, 3:4], verdict[:, 2:3], P, bass.bass_isa.ReduceOp.max)\
                .then_inc(all_bad, 1)

        @block.scalar
        def _(act):
            act.dma_start(W_aug[:, 0:F], W[:, :]).then_inc(w_loaded, 16)
            for c in range(2):
                act.dma_start(a_sb[:, c:c + 1], a[c * F:(c + 1) * F, :]).then_inc(w_loaded, 16)
            act.wait_ge(wT_done, 1)
            nc.scalar.activation(W_T[:, :], ps[:, 1, 0:F], ACT.Copy).then_inc(wT_copied, 1)
            act.wait_ge(wa_done, 1)
            nc.scalar.activation(W_aug[:, F:F + 2], ps[:, 3, 0:2], ACT.Copy).then_inc(wa_copied, 1)
            act.wait_ge(var_ready, 1)
            nc.scalar.activation(std[:, :], var_eps[:, :], ACT.Sqrt).then_inc(std_ready, 1)
            def evacuate(it):
                s = it.chunk % EVACUATED
                if it.kind != OUTPUT:
                    act.wait_ge(transposed, it.n + 1)
                    if it.chunk >= EVACUATED:
                        act.wait_ge(multiplied, it.chunk - EVACUATED + 1)
                        if chunks[it.chunk - EVACUATED].kind == PRODUCT:
                            act.wait_ge(checked, chunks[it.chunk - EVACUATED].product + 1)
                if it.kind == MASKED:
                    nc.scalar.activation(mask[:, s, :], ps[:, it.bank, :].bitcast(BF16), ACT.Copy).then_inc(first_read, 1)
                elif it.kind == PRODUCT:
                    nc.scalar.activation(high[:, s, :], ps[:, it.bank:it.bank + 2, :].rearrange("p b n -> p (b n)"),
                                         ACT.Copy).then_inc(first_read, 1)
                    act.wait_ge(first_read, it.chunk + 1)
                    nc.scalar.activation(mask[:, s, :], high[:, s, :].bitcast(FP32), ACT.Sign).then_inc(act_masked, 1)

            def normalize(g):
                for t in range(g * GRP, (g + 1) * GRP):
                    done = nc.scalar.activation(xn[:, t, :], x_sb[:, t, :], ACT.Relu, bias=mean_rstd[:, t:t + 1],
                                                scale=rstd[:, t:t + 1])
                done.then_inc(xn_ready[g], 1)

            def copy_hT(g):
                act.wait_ge(hT_done, g + 1)
                if g >= 2:
                    act.wait_ge(hw_done, g - 1)
                nc.scalar.activation(hT[:, g % 2, :], ps[:, 1 + 2 * (g % 2), :], ACT.Relu).then_inc(hT_copied, 1)

            act.wait_ge(norm_ready, 1)
            normalize(1)
            evacuate(items[0])
            copy_hT(0)
            normalize(3)
            copy_hT(1)
            normalize(4)
            copy_hT(2)
            evacuate(items[1])
            copy_hT(3)
            copy_hT(4)
            evacuate(items[2])
            copy_hT(5)
            copy_hT(6)
            evacuate(items[3])
            copy_hT(7)

            for it in items:
                if it.n >= EARLY_EVACUATED:
                    evacuate(it)
                if it.n in fs:
                    q = fs[it.n].q
                    act.wait_ge(scores_ready, q + 1)
                    if q >= 1:
                        act.wait_ge(cols_ready, q)
                    nc.scalar.activation(f_quad[:, :], scores[:, :], ACT.Exp).then_inc(f_ready, 1)
                    act.wait_ge(f_ready, q + 1)
                    for k in range(QT):
                        done = nc.scalar.activation(G_high[:, q * QT + k, :], hw[:, q * QT + k, :], ACT.Copy,
                                                    scale=f_quad[:, k:k + 1])
                    done.then_inc(G_high_ready, 1)

        @block.tensor
        def _(pe):
            pe.wait_ge(const_ready, 3)
            pe.wait_ge(w_loaded, 48)
            nc.tensor.transpose(ps[:, 1, 0:F], W_aug[:, 0:F], ident[:, :]).then_inc(wT_done, 1)
            pe.wait_ge(wT_copied, 1)
            nc.tensor.matmul(ps[:, 3, 0:2], W_T[:, :], a_sb[:, :], start=True, stop=True).then_inc(wa_done, 1)
            pe.wait_ge(wa_copied, 1)

            def project(g):
                pe.wait_ge(hT_copied, g + 1)
                if g >= 2:
                    pe.wait_ge(hw_copied, g - 1)
                for k in range(GRP):
                    b = 4 + 2 * (g % 2) + k // 2
                    o = 256 * (k % 2)
                    mm = nc.tensor.matmul(ps[:, b, o:o + F + 2], hT[:, g % 2, k * P:(k + 1) * P], W_aug[:, :],
                                          start=True, stop=True)
                mm.then_inc(hw_done, 1)

            def wait_released(user):
                if user in visits:
                    pe.wait_ge(visit_posted, user.number + 1)
                elif user.kind == MASKED:
                    pe.wait_ge(first_read, user.chunk + 1)
                else:
                    pe.wait_ge(evacuated, user.evacuated + 1)

            def transpose(it):
                if it.kind == PRODUCT:
                    pe.wait_ge(chunk_loaded[it.chunk % LOADED], 16 * (it.chunk // LOADED + 1))
                elif it.kind == MASKED:
                    pe.wait_ge(row_masked, it.mask + 1)
                else:
                    pe.wait_ge(visit_posted, it.visit.number + 1)
                for user in sorted(it.users_before, key=lambda user: user.n):
                    wait_released(user)
                if it.kind == OUTPUT:
                    for k in range(QT):
                        row = it.visit.q * QT + k
                        tr = nc.tensor.transpose(ps[:, it.bank, k * P:(k + 1) * P], product_T[:, row * P:(row + 1) * P],
                                                 ident[:, :])
                else:
                    for j in range(CB):
                        for k in range(QT):
                            at = slice(k * CW + j * P, k * CW + (j + 1) * P)
                            to = j * QW + k * P
                            if it.kind == PRODUCT:
                                tr = nc.tensor.transpose(ps[:, it.bank + to // 512, to % 512:to % 512 + P],
                                                         loaded_rows[:, it.chunk % LOADED, at], ident[:, :])
                            else:
                                tr = nc.tensor.transpose(ps[:, it.bank, :].bitcast(BF16)[:, to:to + P],
                                                         row_mask[:, it.mask % MASKS, at], ident_bf[:, :])
                tr.then_inc(transposed, 1)

            def transpose_xn(g):
                pe.wait_ge(xn_ready[g], 1)
                if g >= 2:
                    pe.wait_ge(hT_copied, g - 1)
                for k in range(GRP):
                    tr = nc.tensor.transpose(ps[:, 1 + 2 * (g % 2), k * P:(k + 1) * P], xn[:, g * GRP + k, :], ident[:, :])
                tr.then_inc(hT_done, 1)

            early = 0
            for g in range(NG + 1):
                if g % 2 == 0 and early < EARLY_TRANSPOSED:
                    for it in items[early:max(early + 1, 2)]:
                        transpose(it)
                        early += 1
                if g < NG:
                    transpose_xn(g)
                if g >= 1:
                    project(g - 1)
            for it in items[early:EARLY_TRANSPOSED]:
                transpose(it)
            pe.wait_ge(hw_copied, NG)
            pe.wait_ge(u_ready, 1)

            def multiply(it):
                visit = it.visit
                c, s = it.columns, it.chunk % EVACUATED
                if it.pos == 0 and visit.number >= 2:
                    pe.wait_ge(visit_posted, visit.number - 1)
                if it is visit.first_product and visit.user_before:
                    wait_released(visit.user_before)
                if it.kind == MASKED:
                    pe.wait_ge(first_read, it.chunk + 1)
                else:
                    pe.wait_ge(evacuated, it.evacuated + 1)
                    pe.wait_ge(G_ready, c * CB // QT + 1 + FREE_QUAD)
                    for j in range(CB):
                        at = slice(j * QW, (j + 1) * QW)
                        b = c * CB + j
                        for m, (left, right) in enumerate(((G_high, high), (G_low, high), (G_high, low))):
                            nc.tensor.matmul(ps[:, visit.product_bank, :], left[:, b, :], right[:, s, at],
                                             start=it is visit.first_product and j == 0 and m == 0,
                                             stop=it is visit.last_product and j == CB - 1 and m == 2)
                    pe.wait_ge(cols_ready, c * CB // QT + 1)
                    pe.wait_ge(act_masked, it.product + 1)
                if visit.kind != SCORES:
                    used = F_COLS
                else:
                    used = slice(0 if it.kind == PRODUCT else U_COLS.start, N_COLS)
                for j in range(CB):
                    for k in range(QT):
                        at = slice(j * QW + k * P, j * QW + (k + 1) * P)
                        mm = nc.tensor.matmul(ps[:, visit.sums_bank, k * 8 + used.start:k * 8 + used.stop], mask[:, s, at],
                                              cols[:, c * CB + j, used], start=it.pos == 0 and j == 0 and k == 0,
                                              stop=it.pos == visit.chunks - 1 and j == CB - 1, skip_group_check=True)
                mm.then_inc(multiplied, 1)

            last = items[-1]
            for it in items:
                if EARLY_TRANSPOSED <= it.n + AHEAD < last.n:
                    transpose(items[it.n + AHEAD])
                if it.kind != OUTPUT:
                    multiply(it)
            transpose(last)

        @block.vector
        def _(v):
            steps = [0]

            def link(ins, step=None):
                if step is None:
                    steps[0] += 1
                    step = steps[0]
                ins.then_inc(dve_step, 1)
                v.wait_ge(dve_step, step)

            nc.vector.memset(cols[:, :, ONE_COL], 1.0)
            for g in range(T // XG):
                v.wait_ge(x_loaded[g], 16)
                for t in range(g * XG, (g + 1) * XG):
                    last = nc.vector.bn_stats(stats[:, t, :], x_sb[:, t, :])
            link(last)
            for t in range(T):
                last = nc.vector.bn_aggr(mv[:, t, :], stats[:, t, :])
            link(last)
            nc.vector.tensor_scalar(var_eps[:, :], mv[:, :, 1], EPS, None, ALU.add).then_inc(var_ready, 1)

            masked = [it for it in items if it.kind == MASKED]

            def mask_rows(it):
                v.wait_ge(chunk_loaded[it.chunk % LOADED], 16 * (it.chunk // LOADED + 1))
                if it.mask >= MASKS:
                    v.wait_ge(transposed, masked[it.mask - MASKS].n + 1)
                nc.vector.tensor_scalar(row_mask[:, it.mask % MASKS, :], loaded_rows[:, it.chunk % LOADED, :],
                                        0.0, None, ALU.is_gt).then_inc(row_masked, 1)

            def copy_hw(g):
                v.wait_ge(hw_done, g + 1)
                b = 4 + 2 * (g % 2)
                src = ps[:, b:b + 2, :].rearrange("p b (h c) -> p (b h) c", h=2)
                nc.vector.tensor_copy(hw[:, g * GRP:(g + 1) * GRP, :], src[:, :, 0:F])
                nc.vector.tensor_copy(uv[:, g * GRP:(g + 1) * GRP, :], src[:, :, F:F + 2]).then_inc(hw_copied, 1)

            mask_rows(masked[0])
            mask_rows(masked[1])
            v.wait_ge(std_ready, 1)
            link(nc.vector.reciprocal(rstd0[:, :], std[:, :]))
            link(nc.vector.tensor_tensor(newton[:, :], rstd0[:, :], rstd0[:, :], ALU.mult))
            link(nc.vector.tensor_tensor(newton[:, :], newton[:, :], var_eps[:, :], ALU.mult))
            link(nc.vector.tensor_scalar(newton[:, :], newton[:, :], -0.5, 1.5, ALU.mult, ALU.add))
            link(nc.vector.tensor_tensor(rstd[:, :], rstd0[:, :], newton[:, :], ALU.mult))
            nc.vector.scalar_tensor_tensor(mean_rstd[:, :], mv[:, :, 0], -1.0, rstd[:, :], ALU.mult, ALU.mult)\
                .then_inc(norm_ready, 1)
            for g in NORM_DVE:
                for t in range(g * GRP, (g + 1) * GRP):
                    last = nc.vector.tensor_scalar(xn[:, t, :], x_sb[:, t, :], mv[:, t, 0:1], rstd[:, t:t + 1],
                                                   ALU.subtract, ALU.mult)
                last.then_inc(xn_ready[g], 1)
            mask_rows(masked[2])
            mask_rows(masked[3])
            copy_hw(0)
            copy_hw(1)
            mask_rows(masked[4])
            copy_hw(2)
            copy_hw(3)
            mask_rows(masked[5])
            copy_hw(4)
            mask_rows(masked[6])
            copy_hw(5)
            mask_rows(masked[7])
            copy_hw(6)
            copy_hw(7)
            v.wait_ge(hw_copied, NG)
            rest = uv[:, :, 0]
            for k in range(3):
                part = cols[:, :, U_COLS.start + k]
                copied = nc.vector.tensor_copy(part, rest)
                if k < 2:
                    link(copied)
                    link(nc.vector.tensor_tensor(u_rest[:, k, :], rest, part, ALU.subtract))
                    rest = u_rest[:, k, :]
                else:
                    copied.then_inc(u_ready, 1)

            def post(visit):
                q = visit.q
                rows = slice(q * QT, (q + 1) * QT)
                mask_sums = ps[:, visit.sums_bank, 0:8 * QT].rearrange("p (k c) -> p k c", c=8)
                all_T = product_T[:, q * QW:(q + 1) * QW]
                v.wait_ge(multiplied, visit.chunks_done)
                if visit.kind == SCORES:
                    link(nc.vector.tensor_reduce(small[:, :], mask_sums[:, :, U_COLS], AX.X, ALU.add))
                    link(nc.vector.scalar_tensor_tensor(e_plus[:, rows], small[:, :], ALPHA, small[:, :],
                                                        ALU.mult, ALU.max))
                    if q == 0:
                        nc.vector.reduce_max(first_max[:, :], e_plus[:, rows], AX.X).then_inc(first_max_ready, 1)
                        v.wait_ge(shift_ready, 1)
                    else:
                        v.wait_ge(f_ready, q)
                    nc.vector.tensor_scalar(scores[:, :], e_plus[:, rows], shift[:, 0:1], SCORE_HIGH,
                                            ALU.subtract, ALU.min).then_inc(scores_ready, 1)
                if visit.first_product:
                    product = ps[:, visit.product_bank, :]
                    if visit.kind == FINAL and q:
                        nc.vector.tensor_tensor(all_T, product, all_T, ALU.add)
                    else:
                        nc.vector.tensor_copy(all_T, product)
                if visit.kind == SCORES:
                    used = slice(0 if visit.first_product else U_COLS.start, N_COLS)
                    done = nc.vector.tensor_copy(sums[:, rows, used], mask_sums[:, :, used])
                elif q:
                    done = nc.vector.tensor_tensor(sums[:, rows, F_COLS], mask_sums[:, :, F_COLS],
                                                   sums[:, rows, F_COLS], ALU.add)
                else:
                    done = nc.vector.tensor_copy(sums[:, rows, F_COLS], mask_sums[:, :, F_COLS])
                if visit.kind == FINAL:
                    link(done)
                    link(nc.vector.tensor_reduce(Z[:, rows], sums[:, rows, F_COLS], AX.X, ALU.add))
                    link(nc.vector.tensor_scalar(Z_held[:, rows], Z[:, rows], Z_LOW, None, ALU.max))
                    done = nc.vector.reciprocal(Z_inverse[:, rows], Z_held[:, rows])
                done.then_inc(visit_posted, 1)

            def finish(it):
                s = it.chunk % EVACUATED
                if it.kind == OUTPUT:
                    v.wait_ge(transposed, it.n + 1)
                    v.wait_ge(visit_posted, it.visit.number + 1)
                    if it.number >= 2:
                        v.wait_ge(stored[it.number % 2], 16 * (it.number // 2))
                    for k in range(QT):
                        row = it.visit.q * QT + k
                        done = nc.vector.scalar_tensor_tensor(
                            out_rows_sb[:, it.number % 2, k, :], ps[:, it.bank, k * P:(k + 1) * P],
                            Z_inverse[:, row:row + 1], x_sb[:, row, :], ALU.mult, ALU.add)
                    done.then_inc(out_ready, 1)
                    v.wait_ge(out_ready, it.number + 1)
                    done = nc.vector.memset(small[:, 0:1], 0.0)
                if it.kind == PRODUCT:
                    v.wait_ge(first_read, it.chunk + 1)
                    done = nc.vector.tensor_tensor(low[:, s, :], ps[:, it.bank:it.bank + 2, :].rearrange("p b n -> p (b n)"),
                                                   high[:, s, :].bitcast(FP32), ALU.subtract)
                done.then_inc(evacuated, 1)
                if it.kind == PRODUCT:
                    v.wait_ge(act_masked, it.product + 1)
                    if it.product >= 2:
                        v.wait_ge(checked, it.product - 1)
                    nc.vector.tensor_scalar(unused[:, it.product % 2, :], mask[:, s, :], 1.0, 0.0, ALU.mult, ALU.min,
                                            accum_out=least[:, it.product:it.product + 1]).then_inc(checked, 1)

            for it in items:
                ahead = it.n + MASK_AHEAD
                if EARLY_MASKED <= ahead < len(items) and items[ahead].kind == MASKED:
                    mask_rows(items[ahead])
                if it.kind != MASKED:
                    finish(it)
                for visit in posts.get(it.n, []):
                    post(visit)
                if it.n in gs:
                    q = gs[it.n].q
                    rows = slice(q * QT, (q + 1) * QT)
                    v.wait_ge(G_quad_ready, q + 1)
                    v.wait_ge(G_high_ready, q + 1)
                    nc.vector.tensor_tensor(G_low[:, rows, :], G_quad[:, :, :], G_high[:, rows, :].bitcast(FP32),
                                            ALU.subtract).then_inc(G_ready, 1)

            link(nc.vector.tensor_scalar(check[:, 0, :], Z[:, :], Z_LOW, None, ALU.is_ge))
            nc.vector.tensor_scalar(check[:, 1, :], Z[:, :], Z_HIGH, None, ALU.is_le)
            nc.vector.tensor_scalar(check[:, 2, :], sums[:, :, ONE_COL], 0.0, None, ALU.is_gt)
            link(nc.vector.tensor_reduce(verdict[:, 0:1], least[:, :], AX.X, ALU.min))
            nc.vector.tensor_scalar(verdict[:, 1:2], verdict[:, 0:1], 0.0, None, ALU.is_lt)
            link(nc.vector.tensor_tensor(check[:, 3, :], check[:, 0, :], check[:, 1, :], ALU.mult))
            link(nc.vector.tensor_tensor(check[:, 0, :], check[:, 2, :], check[:, 3, :], ALU.is_gt))
            link(nc.vector.tensor_reduce(verdict[:, 0:1], check[:, 0, :], AX.X, ALU.max))
            nc.vector.tensor_tensor(verdict[:, 2:3], verdict[:, 0:1], verdict[:, 1:2], ALU.max).then_inc(row_bad, 1)
            v.wait_ge(all_bad, 1)
            link(nc.vector.tensor_copy(S.flag[:, :], verdict[:, 3:4]))


def general_path(nc, S, adj, out):
    N = adj.shape[0]
    T, F = S.hw.shape[1], S.hw.shape[2]
    BIG = 2.0 ** 53
    GRP = 4
    NG = T // GRP
    hw, uv, x_sb, ident, ones = S.hw, S.uv, S.x_sb, S.ident, S.ones
    out_rows = out.rearrange("(t p) f -> p t f", p=P)
    adj_rows = adj.rearrange("(t p) n -> p t n", p=P)

    with ExitStack() as ctx:
        def sb(name, shape, dt=FP32):
            return ctx.enter_context(nc.sbuf_tensor(name, shape, dt))

        def sem(name):
            return ctx.enter_context(nc.semaphore(name))

        bcast = sb("bcast", [P, 2, N])
        row = sb("row", [P, N])
        t1 = sb("t1", [P, N])
        t2 = sb("t2", [P, N])
        prob = sb("prob", [P, N])
        probT = sb("probT", [P, N])
        diag = sb("diag", [P, 2, P])
        part = sb("part", [P, 4])
        e_raw = sb("e_raw", [P, T, 2])
        e_sc = sb("e_sc", [P, T, 2])
        stat = sb("stat", [P, 4])
        out_t = sb("out_t", [P, F])
        gps = ctx.enter_context(nc.psum_tensor("gps", [P, 8, 512], FP32))
        g_diag = sem("g_diag")
        g_bc = sem("g_bc")
        g_row = sem("g_row")
        g_rowused = sem("g_rowused")
        g_dve = sem("g_dve")
        g_t = sem("g_t")
        g_p = sem("g_p")
        g_q = sem("g_q")
        g_qT = sem("g_qT")
        g_qTc = sem("g_qTc")
        g_prod = sem("g_prod")
        g_out = sem("g_out")
        g_stored = sem("g_stored")
        block = ctx.enter_context(nc.Block())

        def flagged(engine):
            return engine.value_load(S.flag[0:1, 0:1], min_val=0, max_val=1)

        @block.sync
        def _(sp):
            with sp.If(flagged(sp)):
                with sp.Fori(0, T) as i:
                    sp.wait_ge(g_rowused, i + 1)
                    sp.dma_start(row[:, :], adj_rows[:, bass.ds(i, 1), :].rearrange("p a n -> p (a n)")).then_inc(g_row, 16)
                with sp.Fori(0, T) as i:
                    sp.wait_ge(g_rowused, i + 1 + T)
                    sp.dma_start(row[:, :], adj_rows[:, bass.ds(i, 1), :].rearrange("p a n -> p (a n)")).then_inc(g_row, 16)
                    sp.wait_ge(g_out, i + 1)
                    sp.dma_start(out_rows[:, bass.ds(i, 1), :], out_t[:, :].rearrange("p (a f) -> p a f", a=1)).then_inc(g_stored, 16)
                sp.wait_ge(g_stored, 16 * T)

        @block.scalar
        def _(act):
            with act.If(flagged(act)):
                with act.Fori(0, T) as i:
                    act.wait_ge(g_t, i + 1)
                    nc.scalar.activation(prob[:, :], t1[:, :], ACT.Exp, bias=stat[:, 1:2], scale=-BIG,
                                         accum_out=stat[:, 2:3]).then_inc(g_p, 1)
                    for g in range(NG):
                        act.wait_ge(g_qT, i * NG + g + 1)
                        nc.scalar.activation(probT[:, g * 512:(g + 1) * 512], gps[:, g % 4, :],
                                             ACT.Copy).then_inc(g_qTc, 1)

        @block.tensor
        def _(pe):
            with pe.If(flagged(pe)):
                for r in range(2):
                    with pe.Fori(0, T) as i:
                        pe.wait_ge(g_diag, i + 1 + r * T)
                        for c in range(2):
                            mm = nc.tensor.matmul(gps[:, c, 0:P], ones[:, :], diag[:, c, :], start=True, stop=True)
                        mm.then_inc(g_bc, 1)
                with pe.Fori(0, T) as i:
                    pe.wait_ge(g_q, i + 1)
                    for g in range(NG):
                        if g >= 4:
                            pe.wait_ge(g_qTc, i * NG + g - 3)
                        for k in range(GRP):
                            b = g * GRP + k
                            tr = nc.tensor.transpose(gps[:, g % 4, k * P:(k + 1) * P], t2[:, b * P:(b + 1) * P], ident[:, :])
                        tr.then_inc(g_qT, 1)
                    pe.wait_ge(g_qTc, i * NG + NG)
                    for b in range(T):
                        mm = nc.tensor.matmul(gps[:, 5, 0:F], probT[:, b * P:(b + 1) * P], hw[:, b, :],
                                              start=b == 0, stop=b == T - 1)
                    mm.then_inc(g_prod, 1)

        @block.vector
        def _(v):
            with v.If(flagged(v)):
                m = [0]

                def glink(ins, i, K, j):
                    ins.then_inc(g_dve, 1)
                    v.wait_ge(g_dve, m[0] + i * K + j)

                def broadcast(src, r):
                    with v.Fori(0, T) as i:
                        glink(nc.vector.tensor_copy(part[:, 0:2], src[:, bass.ds(i, 1), :].rearrange("p a c -> p (a c)")), i, 2, 1)
                        for c in range(2):
                            d = nc.vector.tensor_scalar(diag[:, c, :], ident[:, :], part[:, c:c + 1], None, ALU.mult)
                        d.then_inc(g_diag, 1)
                        v.wait_ge(g_bc, i + 1 + r * T)
                        glink(nc.vector.tensor_copy(bcast[:, :, bass.ds(i * P, P)], gps[:, 0:2, 0:P]), i, 2, 2)
                    m[0] += 2 * T

                broadcast(uv, 0)
                nc.vector.memset(part[:, :], 0.0).then_inc(g_rowused, 1)
                with v.Fori(0, T) as i:
                    v.wait_ge(g_row, i * 16 + 16)
                    for k, (cmp, c) in enumerate(((ALU.is_gt, 0), (ALU.is_lt, 1), (ALU.is_lt, 0), (ALU.is_gt, 1))):
                        last = nc.vector.scalar_tensor_tensor(t1[:, :], row[:, :], 0.0, bcast[:, c, :], cmp, ALU.mult,
                                                              accum_out=part[:, k:k + 1])
                        if k < 3:
                            glink(last, i, 5, k + 1)
                    last.then_inc(g_rowused, 1)
                    v.wait_ge(g_rowused, i + 2)
                    glink(nc.vector.tensor_reduce(stat[:, 0:2], part[:, :].rearrange("p (s k) -> p s k", k=2), AX.X, ALU.add), i, 5, 4)
                    glink(nc.vector.scalar_tensor_tensor(e_raw[:, bass.ds(i, 1), :].rearrange("p a c -> p (a c)"), stat[:, 0:2], ALPHA,
                                                         stat[:, 0:2], ALU.mult, ALU.max), i, 5, 5)
                m[0] += 5 * T
                glink(nc.vector.tensor_scalar(e_sc[:, :, :], e_raw[:, :, :], 1.0 / BIG, None, ALU.mult), 0, 0, 1)
                m[0] += 1
                broadcast(e_sc, 1)
                with v.Fori(0, T) as i:
                    v.wait_ge(g_row, i * 16 + 16 + 16 * T)
                    nc.vector.scalar_tensor_tensor(t1[:, :], row[:, :], 0.0, bcast[:, 0, :], ALU.is_le, ALU.subtract)
                    glink(nc.vector.scalar_tensor_tensor(t2[:, :], row[:, :], 0.0, bcast[:, 1, :], ALU.is_ge, ALU.subtract), i, 5, 1)
                    glink(nc.vector.tensor_tensor(t1[:, :], t1[:, :], t2[:, :], ALU.min), i, 5, 2)
                    glink(nc.vector.tensor_reduce(stat[:, 0:1], t1[:, :], AX.X, ALU.min), i, 5, 3)
                    nc.vector.tensor_scalar(stat[:, 1:2], stat[:, 0:1], BIG, None, ALU.mult).then_inc(g_t, 1)
                    v.wait_ge(g_p, i + 1)
                    nc.vector.tensor_tensor(t2[:, :], prob[:, :], row[:, :], ALU.mult).then_inc(g_q, 1)
                    v.wait_ge(g_q, i + 1)
                    glink(nc.vector.reciprocal(stat[:, 3:4], stat[:, 2:3]), i, 5, 4)
                    glink(nc.vector.tensor_copy(part[:, 0:1], stat[:, 3:4]), i, 5, 5)
                    nc.vector.memset(part[:, 1:2], 0.0).then_inc(g_rowused, 1)
                    v.wait_ge(g_prod, i + 1)
                    nc.vector.scalar_tensor_tensor(out_t[:, :], gps[:, 5, 0:F], stat[:, 3:4],
                                                   x_sb[:, bass.ds(i, 1), :].rearrange("p a f -> p (a f)"),
                                                   ALU.mult, ALU.add).then_inc(g_out, 1)
                    v.wait_ge(g_stored, i * 16 + 16)



def build(nc, x, adj, W, a, out):
    N, F = x.shape
    with ExitStack() as ctx:
        S = shared_tensors(nc, ctx, N // P, F)
        main_path(nc, S, x, adj, W, a, out)
        general_path(nc, S, adj, out)


_INS = ['x', 'adj', 'L0_gnn_W', 'L0_gnn_a']


def kernel(**inputs):
    import concourse.bacc as bacc
    from concourse.bass_utils import run_bass_kernel_spmd as run

    nc = bacc.Bacc("TRN2", target_bir_lowering=False, num_devices=1)
    arrays, args = {}, []
    for name in _INS:
        arr = np.ascontiguousarray(inputs[name])
        arrays[f"in_{name}"] = arr
        args.append(nc.dram_tensor(f"in_{name}", arr.shape, mybir.dt.from_np(arr.dtype), kind="ExternalInput").ap())
    out = nc.dram_tensor("out_0", inputs["x"].shape, mybir.dt.float32, kind="ExternalOutput").ap()
    build(nc, *args, out)
    res = run(nc, [arrays], core_ids=[0])
    return res.results[0]["out_0"]
```
